# Optimizing a Trainium2 kernel written in Bass

```python
import numpy as np
import jax
import jax.numpy as jnp

def _softmax(x, axis=-1):
    return jax.nn.softmax(x, axis=axis)

def _gelu(x):
    return jax.nn.gelu(x, approximate=True)

def _silu(x):
    return jax.nn.silu(x)

def _sigmoid(x):
    return jax.nn.sigmoid(x)

def _layernorm(x, axis=-1, eps=1e-05):
    m = jnp.mean(x, axis=axis, keepdims=True)
    v = jnp.var(x, axis=axis, keepdims=True)
    return (x - m) / jnp.sqrt(v + eps)

def _scatter_add(tgt, idx, src, axis=0):
    return tgt.at[idx].add(src)

def _segment_sum(src, seg, n):
    return jax.ops.segment_sum(src, seg, n)
kernel_name = 'mk_gps_d2_gnn_r8_85b6b7'

def setup_inputs(seed: int=0):
    np.random.seed(seed)
    _w = jnp.asarray

    def _rec_inputs():
        import jax
        import jax.numpy as jnp
        _gk = jax.random.key(seed)
        x = -0.0001126 + 1 * jax.random.normal(jax.random.fold_in(_gk, 1), (1250, 768), jnp.float32)
        src = jax.random.randint(jax.random.fold_in(_gk, 2), (20000,), 0, 1250, jnp.int32)
        dst = jnp.minimum((1250 * jax.random.uniform(jax.random.fold_in(_gk, 3), (20000,)) ** 2.0).astype(jnp.int32), 9999)
        _o = jnp.argsort(dst, stable=True)
        src = src[_o]
        dst = dst[_o]
        return (x, src, dst)
    x, src, dst = _rec_inputs()

    def _L0_gnn_setup():
        import jax, jax.numpy as jnp
        import numpy as np
        N_NODES = 1250
        key = jax.random.key(seed)
        k1, k2, k3 = jax.random.split(key, 3)
        x = jax.random.normal(k1, (N_NODES, 768), dtype=jnp.float32)
        edge_index = jax.random.randint(k2, (2, 12500), 0, N_NODES, dtype=jnp.int32)
        W = jax.random.normal(k3, (768, 768), dtype=jnp.float32) * (1.0 / np.sqrt(768))
        b = jnp.zeros((768,), dtype=jnp.float32)
        return {'x': x, 'edge_index': edge_index, 'W': W, 'b': b}
    _L0_gnn_all = _L0_gnn_setup()
    _L0_gnn_in = {k: v for k, v in _L0_gnn_all.items() if k in ('W', 'b')}
    del _L0_gnn_all

    def _L0_mix_setup():
        import jax, jax.numpy as jnp
        import numpy as np
        EPS = 0.0001
        LN_EPS = 1e-05

        def _layernorm(x, g, b):
            m = jnp.mean(x, axis=-1, keepdims=True)
            v = jnp.mean(jnp.square(x - m), axis=-1, keepdims=True)
            return (x - m) * jax.lax.rsqrt(v + LN_EPS) * g + b

        def _softmax_features(x, proj, is_query):
            d = x.shape[-1]
            xn = x * d ** (-0.25)
            u = jnp.einsum('bhnd,md->bhnm', xn, proj)
            diag = 0.5 * jnp.sum(jnp.square(xn), axis=-1, keepdims=True)
            if is_query:
                stab = jnp.max(u, axis=-1, keepdims=True)
            else:
                stab = jnp.max(u, axis=(-2, -1), keepdims=True)
            ratio = proj.shape[0] ** (-0.5)
            return ratio * (jnp.exp(u - diag - stab) + EPS)
        B, N, E, H, M, F = (4, 256, 768, 12, 256, 384)
        Dh = E // H
        key = jax.random.key(seed)
        ks = jax.random.split(key, 4)
        return {'x': jax.random.normal(ks[0], (B, N, E), jnp.float32), 'proj': jax.random.normal(ks[1], (M, Dh), jnp.float32), 'ln1_g': jnp.ones((E,), jnp.float32), 'ln1_b': jnp.zeros((E,), jnp.float32), 'ln2_g': jnp.ones((E,), jnp.float32), 'ln2_b': jnp.zeros((E,), jnp.float32), 'W1': jax.random.normal(ks[2], (E, F), jnp.float32) * 0.02, 'b1': jnp.zeros((F,), jnp.float32), 'W2': jax.random.normal(ks[3], (F, E), jnp.float32) * 0.02, 'b2': jnp.zeros((E,), jnp.float32)}
    _L0_mix_all = _L0_mix_setup()
    _L0_mix_in = {k: v for k, v in _L0_mix_all.items() if k in ('proj', 'ln1_g', 'ln1_b', 'ln2_g', 'ln2_b', 'W1', 'b1', 'W2', 'b2')}
    del _L0_mix_all

    def _L0_ffn_setup():
        import jax, jax.numpy as jnp
        import numpy as np
        TOPK = 2

        def _moe_forward(x, router_w, w_fc, b_fc, w_proj, b_proj):
            B, S, D = x.shape
            E = router_w.shape[0]
            xt = x.reshape(-1, D)
            gate_logits = xt @ router_w.T
            weights, selected = jax.lax.top_k(gate_logits, TOPK)
            weights = jax.nn.softmax(weights.astype(jnp.float32), axis=1).astype(x.dtype)
            onehot = jax.nn.one_hot(selected, E, dtype=x.dtype)
            comb = jnp.einsum('tk,tke->te', weights, onehot)
            h = jax.nn.gelu(jnp.einsum('td,edf->etf', xt, w_fc) + b_fc[:, None, :], approximate=False)
            y = jnp.einsum('etf,efd->etd', h, w_proj) + b_proj[:, None, :]
            out = jnp.einsum('te,etd->td', comb, y)
            return out.reshape(B, S, D)
        key = jax.random.key(seed)
        ks = jax.random.split(key, 4)
        B, S, D, F, E = (4, 1024, 768, 384, 8)
        scale_in = 1.0 / np.sqrt(D)
        scale_hid = 1.0 / np.sqrt(F)
        return {'x': jax.random.normal(ks[0], (B, S, D), dtype=jnp.float32), 'router_w': jax.random.normal(ks[1], (E, D), dtype=jnp.float32) * scale_in, 'w_fc': jax.random.normal(ks[2], (E, D, F), dtype=jnp.float32) * scale_in, 'b_fc': jnp.zeros((E, F), dtype=jnp.float32), 'w_proj': jax.random.normal(ks[3], (E, F, D), dtype=jnp.float32) * scale_hid, 'b_proj': jnp.zeros((E, D), dtype=jnp.float32)}
    _L0_ffn_all = _L0_ffn_setup()
    _L0_ffn_in = {k: v for k, v in _L0_ffn_all.items() if k in ('router_w', 'w_fc', 'b_fc', 'w_proj', 'b_proj')}
    del _L0_ffn_all

    def _L1_gnn_setup():
        import jax, jax.numpy as jnp
        import numpy as np
        N = 6250
        E = 200000
        IN_DIM = 768
        HID = 256
        OUT_DIM = 768
        HEADS = 4
        NEG_SLOPE = 0.2

        def gat_conv(x, src, dst, W, a_src, a_dst, bias, heads):
            n = x.shape[0]
            h = (x @ W).reshape(n, heads, -1)
            alpha_s = (h * a_src[None]).sum(-1)
            alpha_d = (h * a_dst[None]).sum(-1)
            e = jax.nn.leaky_relu(alpha_s[src] + alpha_d[dst], NEG_SLOPE)
            m = jax.ops.segment_max(e, dst, num_segments=n)
            e = jnp.exp(e - m[dst])
            denom = jax.ops.segment_sum(e, dst, num_segments=n)
            alpha = e / (denom[dst] + 1e-16)
            out = jax.ops.segment_sum(h[src] * alpha[:, :, None], dst, num_segments=n)
            return out.reshape(n, -1) + bias
        key = jax.random.key(seed)
        ks = jax.random.split(key, 12)
        C1 = HID // HEADS
        x = jax.random.normal(ks[0], (N, IN_DIM), dtype=jnp.float32)
        edge_index = jax.random.randint(ks[1], (2, E), 0, N, dtype=jnp.int64)
        sc = lambda f: 1.0 / np.sqrt(f)
        W1 = jax.random.normal(ks[2], (IN_DIM, HEADS * C1), jnp.float32) * sc(IN_DIM)
        a_src1 = jax.random.normal(ks[3], (HEADS, C1), jnp.float32) * sc(C1)
        a_dst1 = jax.random.normal(ks[4], (HEADS, C1), jnp.float32) * sc(C1)
        b1 = jnp.zeros((HEADS * C1,), jnp.float32)
        W2 = jax.random.normal(ks[5], (HID, HID), jnp.float32) * sc(HID)
        a_src2 = jax.random.normal(ks[6], (1, HID), jnp.float32) * sc(HID)
        a_dst2 = jax.random.normal(ks[7], (1, HID), jnp.float32) * sc(HID)
        b2 = jnp.zeros((HID,), jnp.float32)
        Wm1 = jax.random.normal(ks[8], (HID, HID), jnp.float32) * sc(HID)
        bm1 = jnp.zeros((HID,), jnp.float32)
        Wm2 = jax.random.normal(ks[9], (HID, OUT_DIM), jnp.float32) * sc(HID)
        bm2 = jnp.zeros((OUT_DIM,), jnp.float32)
        return {'x': x, 'edge_index': edge_index, 'W1': W1, 'a_src1': a_src1, 'a_dst1': a_dst1, 'b1': b1, 'W2': W2, 'a_src2': a_src2, 'a_dst2': a_dst2, 'b2': b2, 'Wm1': Wm1, 'bm1': bm1, 'Wm2': Wm2, 'bm2': bm2}
    _L1_gnn_all = _L1_gnn_setup()
    _L1_gnn_in = {k: v for k, v in _L1_gnn_all.items() if k in ('W1', 'a_src1', 'a_dst1', 'b1', 'W2', 'a_src2', 'a_dst2', 'b2', 'Wm1', 'bm1', 'Wm2', 'bm2')}
    del _L1_gnn_all

    def _L1_mix_setup():
        import jax, jax.numpy as jnp
        import numpy as np
        LN_EPS = 1e-05
        NORM_EPS = 1e-12

        def _layernorm(x, gamma, beta):
            mu = jnp.mean(x, axis=-1, keepdims=True)
            var = jnp.mean(jnp.square(x - mu), axis=-1, keepdims=True)
            return (x - mu) * jax.lax.rsqrt(var + LN_EPS) * gamma + beta

        def _l2norm(x):
            n = jnp.sqrt(jnp.sum(jnp.square(x), axis=-1, keepdims=True))
            return x / jnp.maximum(n, NORM_EPS)
        key = jax.random.key(seed)
        ks = jax.random.split(key, 4)
        B, N, C, E = (8, 512, 768, 768)
        x = jax.random.normal(ks[0], (B, N, C), dtype=jnp.float32)
        w_qkv = jax.random.normal(ks[1], (C, 3 * E), dtype=jnp.float32) * (1.0 / np.sqrt(C))
        w_proj = jax.random.normal(ks[2], (E, C), dtype=jnp.float32) * (1.0 / np.sqrt(E))
        ln_in_g = jnp.ones((C,), jnp.float32)
        ln_in_b = jnp.zeros((C,), jnp.float32)
        ln_out_g = jnp.ones((E,), jnp.float32)
        ln_out_b = jnp.zeros((E,), jnp.float32)
        return {'x': x, 'w_qkv': w_qkv, 'w_proj': w_proj, 'ln_in_g': ln_in_g, 'ln_in_b': ln_in_b, 'ln_out_g': ln_out_g, 'ln_out_b': ln_out_b}
    _L1_mix_all = _L1_mix_setup()
    _L1_mix_in = {k: v for k, v in _L1_mix_all.items() if k in ('w_qkv', 'w_proj', 'ln_in_g', 'ln_in_b', 'ln_out_g', 'ln_out_b')}
    del _L1_mix_all

    def _L1_ffn_setup():
        import jax, jax.numpy as jnp
        import numpy as np
        B, T, E = (2, 1024, 768)
        H = 384
        N_EXP = 4
        key = jax.random.key(seed)
        ks = jax.random.split(key, 8)
        s_e = 1.0 / np.sqrt(E)
        s_h = 1.0 / np.sqrt(H)
        return {'x': jax.random.normal(ks[0], (B, T, E), dtype=jnp.float32), 'Wg': jax.random.uniform(ks[1], (E, N_EXP), minval=-s_e, maxval=s_e, dtype=jnp.float32), 'bg': jax.random.uniform(ks[2], (N_EXP,), minval=-s_e, maxval=s_e, dtype=jnp.float32), 'W1': jax.random.uniform(ks[3], (N_EXP, E, H), minval=-s_e, maxval=s_e, dtype=jnp.float32), 'b1': jax.random.uniform(ks[4], (N_EXP, H), minval=-s_e, maxval=s_e, dtype=jnp.float32), 'W2': jax.random.uniform(ks[5], (N_EXP, H, E), minval=-s_h, maxval=s_h, dtype=jnp.float32), 'b2': jax.random.uniform(ks[6], (N_EXP, E), minval=-s_h, maxval=s_h, dtype=jnp.float32)}
    _L1_ffn_all = _L1_ffn_setup()
    _L1_ffn_in = {k: v for k, v in _L1_ffn_all.items() if k in ('Wg', 'bg', 'W1', 'b1', 'W2', 'b2')}
    del _L1_ffn_all
    return {'x': x, 'src': src, 'dst': dst, 'L0_gnn_W': _L0_gnn_in['W'], 'L0_gnn_b': _L0_gnn_in['b'], 'L0_mix_proj': _L0_mix_in['proj'], 'L0_mix_ln1_g': _L0_mix_in['ln1_g'], 'L0_mix_ln1_b': _L0_mix_in['ln1_b'], 'L0_mix_ln2_g': _L0_mix_in['ln2_g'], 'L0_mix_ln2_b': _L0_mix_in['ln2_b'], 'L0_mix_W1': _L0_mix_in['W1'], 'L0_mix_b1': _L0_mix_in['b1'], 'L0_mix_W2': _L0_mix_in['W2'], 'L0_mix_b2': _L0_mix_in['b2'], 'L0_ffn_router_w': _L0_ffn_in['router_w'], 'L0_ffn_w_fc': _L0_ffn_in['w_fc'], 'L0_ffn_b_fc': _L0_ffn_in['b_fc'], 'L0_ffn_w_proj': _L0_ffn_in['w_proj'], 'L0_ffn_b_proj': _L0_ffn_in['b_proj'], 'L1_gnn_W1': _L1_gnn_in['W1'], 'L1_gnn_a_src1': _L1_gnn_in['a_src1'], 'L1_gnn_a_dst1': _L1_gnn_in['a_dst1'], 'L1_gnn_b1': _L1_gnn_in['b1'], 'L1_gnn_W2': _L1_gnn_in['W2'], 'L1_gnn_a_src2': _L1_gnn_in['a_src2'], 'L1_gnn_a_dst2': _L1_gnn_in['a_dst2'], 'L1_gnn_b2': _L1_gnn_in['b2'], 'L1_gnn_Wm1': _L1_gnn_in['Wm1'], 'L1_gnn_bm1': _L1_gnn_in['bm1'], 'L1_gnn_Wm2': _L1_gnn_in['Wm2'], 'L1_gnn_bm2': _L1_gnn_in['bm2'], 'L1_mix_w_qkv': _L1_mix_in['w_qkv'], 'L1_mix_w_proj': _L1_mix_in['w_proj'], 'L1_mix_ln_in_g': _L1_mix_in['ln_in_g'], 'L1_mix_ln_in_b': _L1_mix_in['ln_in_b'], 'L1_mix_ln_out_g': _L1_mix_in['ln_out_g'], 'L1_mix_ln_out_b': _L1_mix_in['ln_out_b'], 'L1_ffn_Wg': _L1_ffn_in['Wg'], 'L1_ffn_bg': _L1_ffn_in['bg'], 'L1_ffn_W1': _L1_ffn_in['W1'], 'L1_ffn_b1': _L1_ffn_in['b1'], 'L1_ffn_W2': _L1_ffn_in['W2'], 'L1_ffn_b2': _L1_ffn_in['b2']}

def reference(x, src, dst, L0_gnn_W, L0_gnn_b, L0_mix_proj, L0_mix_ln1_g, L0_mix_ln1_b, L0_mix_ln2_g, L0_mix_ln2_b, L0_mix_W1, L0_mix_b1, L0_mix_W2, L0_mix_b2, L0_ffn_router_w, L0_ffn_w_fc, L0_ffn_b_fc, L0_ffn_w_proj, L0_ffn_b_proj, L1_gnn_W1, L1_gnn_a_src1, L1_gnn_a_dst1, L1_gnn_b1, L1_gnn_W2, L1_gnn_a_src2, L1_gnn_a_dst2, L1_gnn_b2, L1_gnn_Wm1, L1_gnn_bm1, L1_gnn_Wm2, L1_gnn_bm2, L1_mix_w_qkv, L1_mix_w_proj, L1_mix_ln_in_g, L1_mix_ln_in_b, L1_mix_ln_out_g, L1_mix_ln_out_b, L1_ffn_Wg, L1_ffn_bg, L1_ffn_W1, L1_ffn_b1, L1_ffn_W2, L1_ffn_b2):
    import jax
    import jax.numpy as jnp

    def _L0_gnn_ref(x, edge_index, W, b):
        import jax, jax.numpy as jnp
        import numpy as np
        N_NODES = 1250
        n = x.shape[0]
        loops = jnp.arange(n, dtype=edge_index.dtype)
        row = jnp.concatenate([edge_index[0], loops])
        col = jnp.concatenate([edge_index[1], loops])
        ones = jnp.ones(row.shape[0], dtype=x.dtype)
        deg = jax.ops.segment_sum(ones, col, num_segments=n)
        dinv = jnp.where(deg > 0, jax.lax.rsqrt(deg), 0.0)
        norm = dinv[row] * dinv[col]
        h = x @ W
        msg = h[row] * norm[:, None]
        out = jax.ops.segment_sum(msg, col, num_segments=n) + b
        return out

    def _L0_mix_ref(x, proj, ln1_g, ln1_b, ln2_g, ln2_b, W1, b1, W2, b2):
        import jax, jax.numpy as jnp
        import numpy as np
        EPS = 0.0001
        LN_EPS = 1e-05

        def _layernorm(x, g, b):
            m = jnp.mean(x, axis=-1, keepdims=True)
            v = jnp.mean(jnp.square(x - m), axis=-1, keepdims=True)
            return (x - m) * jax.lax.rsqrt(v + LN_EPS) * g + b

        def _softmax_features(x, proj, is_query):
            d = x.shape[-1]
            xn = x * d ** (-0.25)
            u = jnp.einsum('bhnd,md->bhnm', xn, proj)
            diag = 0.5 * jnp.sum(jnp.square(xn), axis=-1, keepdims=True)
            if is_query:
                stab = jnp.max(u, axis=-1, keepdims=True)
            else:
                stab = jnp.max(u, axis=(-2, -1), keepdims=True)
            ratio = proj.shape[0] ** (-0.5)
            return ratio * (jnp.exp(u - diag - stab) + EPS)
        B, N, E = x.shape
        M, Dh = proj.shape
        H = E // Dh
        h = _layernorm(x, ln1_g, ln1_b)
        qkv = h.reshape(B, N, H, Dh).transpose(0, 2, 1, 3)
        q_p = _softmax_features(qkv, proj, is_query=True)
        k_p = _softmax_features(qkv, proj, is_query=False)
        k_sum = jnp.sum(k_p, axis=-2)
        d_inv = 1.0 / jnp.einsum('bhnm,bhm->bhn', q_p, k_sum)
        ctx = jnp.einsum('bhnm,bhnd->bhmd', k_p, qkv)
        attn = jnp.einsum('bhnm,bhmd,bhn->bhnd', q_p, ctx, d_inv)
        attn = attn.transpose(0, 2, 1, 3).reshape(B, N, E)
        x = x + attn
        h2 = _layernorm(x, ln2_g, ln2_b)
        h2 = jax.nn.gelu(h2 @ W1 + b1, approximate=False) @ W2 + b2
        return x + h2

    def _L0_ffn_ref(x, router_w, w_fc, b_fc, w_proj, b_proj):
        import jax, jax.numpy as jnp
        import numpy as np
        TOPK = 2

        def _moe_forward(x, router_w, w_fc, b_fc, w_proj, b_proj):
            B, S, D = x.shape
            E = router_w.shape[0]
            xt = x.reshape(-1, D)
            gate_logits = xt @ router_w.T
            weights, selected = jax.lax.top_k(gate_logits, TOPK)
            weights = jax.nn.softmax(weights.astype(jnp.float32), axis=1).astype(x.dtype)
            onehot = jax.nn.one_hot(selected, E, dtype=x.dtype)
            comb = jnp.einsum('tk,tke->te', weights, onehot)
            h = jax.nn.gelu(jnp.einsum('td,edf->etf', xt, w_fc) + b_fc[:, None, :], approximate=False)
            y = jnp.einsum('etf,efd->etd', h, w_proj) + b_proj[:, None, :]
            out = jnp.einsum('te,etd->td', comb, y)
            return out.reshape(B, S, D)
        return _moe_forward(x, router_w, w_fc, b_fc, w_proj, b_proj)

    def _L1_gnn_ref(x, edge_index, W1, a_src1, a_dst1, b1, W2, a_src2, a_dst2, b2, Wm1, bm1, Wm2, bm2):
        import jax, jax.numpy as jnp
        import numpy as np
        N = 6250
        E = 200000
        IN_DIM = 768
        HID = 256
        OUT_DIM = 768
        HEADS = 4
        NEG_SLOPE = 0.2

        def gat_conv(x, src, dst, W, a_src, a_dst, bias, heads):
            n = x.shape[0]
            h = (x @ W).reshape(n, heads, -1)
            alpha_s = (h * a_src[None]).sum(-1)
            alpha_d = (h * a_dst[None]).sum(-1)
            e = jax.nn.leaky_relu(alpha_s[src] + alpha_d[dst], NEG_SLOPE)
            m = jax.ops.segment_max(e, dst, num_segments=n)
            e = jnp.exp(e - m[dst])
            denom = jax.ops.segment_sum(e, dst, num_segments=n)
            alpha = e / (denom[dst] + 1e-16)
            out = jax.ops.segment_sum(h[src] * alpha[:, :, None], dst, num_segments=n)
            return out.reshape(n, -1) + bias
        n = x.shape[0]
        loops = jnp.arange(n, dtype=edge_index.dtype)
        src = jnp.concatenate([edge_index[0], loops])
        dst = jnp.concatenate([edge_index[1], loops])
        h = gat_conv(x, src, dst, W1, a_src1, a_dst1, b1, HEADS)
        h = jax.nn.relu(h)
        h = gat_conv(h, src, dst, W2, a_src2, a_dst2, b2, 1)
        h = jax.nn.relu(h)
        h = jax.nn.relu(h @ Wm1 + bm1)
        return h @ Wm2 + bm2

    def _L1_mix_ref(x, w_qkv, w_proj, ln_in_g, ln_in_b, ln_out_g, ln_out_b):
        import jax, jax.numpy as jnp
        import numpy as np
        LN_EPS = 1e-05
        NORM_EPS = 1e-12

        def _layernorm(x, gamma, beta):
            mu = jnp.mean(x, axis=-1, keepdims=True)
            var = jnp.mean(jnp.square(x - mu), axis=-1, keepdims=True)
            return (x - mu) * jax.lax.rsqrt(var + LN_EPS) * gamma + beta

        def _l2norm(x):
            n = jnp.sqrt(jnp.sum(jnp.square(x), axis=-1, keepdims=True))
            return x / jnp.maximum(n, NORM_EPS)
        h = _layernorm(x, ln_in_g, ln_in_b)
        qkv = h @ w_qkv
        q, k, v = jnp.split(qkv, 3, axis=-1)
        phi_q = _l2norm(q)
        phi_k = _l2norm(k)
        kv = jnp.sum(phi_k * v, axis=1)
        attn = phi_q * kv[:, None, :]
        out = _layernorm(attn, ln_out_g, ln_out_b) @ w_proj
        return out

    def _L1_ffn_ref(x, Wg, bg, W1, b1, W2, b2):
        import jax, jax.numpy as jnp
        import numpy as np
        B, T, E = (2, 1024, 768)
        H = 384
        N_EXP = 4
        gate_logits = jnp.einsum('bte,en->btn', x, Wg) + bg
        top = jnp.argmax(gate_logits, axis=-1)
        h = jax.nn.gelu(jnp.einsum('bte,neh->nbth', x, W1) + b1[:, None, None, :], approximate=False)
        y = jnp.einsum('nbth,nhe->nbte', h, W2) + b2[:, None, None, :]
        onehot = jax.nn.one_hot(top, N_EXP, dtype=x.dtype)
        out = jnp.einsum('nbte,btn->bte', y, onehot)
        return out
    edge_index = jnp.stack([src, dst])
    xn = _layernorm(x, axis=-1)
    x = x + _L0_gnn_ref(xn, edge_index, L0_gnn_W, L0_gnn_b) + _L0_mix_ref(xn[None], L0_mix_proj, L0_mix_ln1_g, L0_mix_ln1_b, L0_mix_ln2_g, L0_mix_ln2_b, L0_mix_W1, L0_mix_b1, L0_mix_W2, L0_mix_b2)[0]
    x = x + _L0_ffn_ref(_layernorm(x, axis=-1)[None], L0_ffn_router_w, L0_ffn_w_fc, L0_ffn_b_fc, L0_ffn_w_proj, L0_ffn_b_proj)[0]
    xn = _layernorm(x, axis=-1)
    x = x + _L1_gnn_ref(xn, edge_index, L1_gnn_W1, L1_gnn_a_src1, L1_gnn_a_dst1, L1_gnn_b1, L1_gnn_W2, L1_gnn_a_src2, L1_gnn_a_dst2, L1_gnn_b2, L1_gnn_Wm1, L1_gnn_bm1, L1_gnn_Wm2, L1_gnn_bm2) + _L1_mix_ref(xn[None], L1_mix_w_qkv, L1_mix_w_proj, L1_mix_ln_in_g, L1_mix_ln_in_b, L1_mix_ln_out_g, L1_mix_ln_out_b)[0]
    x = x + _L1_ffn_ref(_layernorm(x, axis=-1)[None], L1_ffn_Wg, L1_ffn_bg, L1_ffn_W1, L1_ffn_b1, L1_ffn_W2, L1_ffn_b2)[0]
    return x

_drawn_inputs = setup_inputs


def setup_inputs(seed=0):
    import zlib

    import numpy as np

    out = dict(_drawn_inputs(seed))
    spreads = {'L0_gnn_b': (0.0, 0.1),
     'L0_mix_ln1_g': (1.0, 0.6),
     'L0_mix_ln1_b': (0.0, 0.1),
     'L0_mix_ln2_g': (1.0, 0.2),
     'L0_mix_ln2_b': (0.0, 0.369),
     'L0_mix_b1': (0.0, 0.267),
     'L0_mix_b2': (0.0, 0.1),
     'L0_ffn_b_fc': (0.0, 0.1),
     'L0_ffn_b_proj': (0.0, 0.1),
     'L1_gnn_b1': (0.0, 0.59),
     'L1_gnn_b2': (0.0, 0.332),
     'L1_gnn_bm1': (0.0, 0.1),
     'L1_gnn_bm2': (0.0, 0.1),
     'L1_mix_ln_in_g': (1.0, 0.2),
     'L1_mix_ln_in_b': (0.0, 0.1),
     'L1_mix_ln_out_g': (1.0, 0.2),
     'L1_mix_ln_out_b': (0.0, 0.1)}
    factors = {'L0_mix_proj': 7.445,
     'L1_gnn_W1': 2.677,
     'L1_gnn_a_src1': 4.137,
     'L1_gnn_a_dst1': 8.0,
     'L1_gnn_a_src2': 8.0,
     'L1_gnn_a_dst2': 8.0,
     'L1_ffn_bg': 2.822,
     'L1_ffn_b1': 8.0,
     'L1_ffn_b2': 4.505}
    for name, (base, spread) in spreads.items():
        noise = np.random.default_rng([zlib.crc32(name.encode()), seed]).standard_normal(out[name].shape)
        drawn = base * np.exp(spread * noise) if base else spread * noise
        out[name] = jnp.asarray(drawn.astype(out[name].dtype))
    for name, factor in factors.items():
        out[name] = (out[name] * factor).astype(out[name].dtype)
    return out
```

```python
from contextlib import ExitStack

import concourse.bass as bass
from concourse import mybir

F32 = mybir.dt.float32
BF16 = mybir.dt.bfloat16
F16 = mybir.dt.float16
I32 = mybir.dt.int32
U32 = mybir.dt.uint32
ALU = mybir.AluOpType
ACT = mybir.ActivationFunctionType
AX = mybir.AxisListType

N, D = 1250, 768
PT = 125
NT = N // PT
KD = D // 128
HALF = D // 2
CHUNKS = ((0, 500), (500, 500), (1000, 250))
E = 20000
EC = E // PT
HEADS0, DH0, M0 = 12, 64, 256
F0, EXP0 = 384, 8
KF = F0 // 128
HID, HEADS1 = 256, 4
EXP1 = 4
LN_EPS = 1e-5
EPS0 = 1e-4
SC0 = DH0 ** -0.25
NEG = -1e30


class Chain:

    def __init__(self, eng, sem, base=0):
        self.eng, self.sem, self.base, self.n = eng, sem, base, 0

    def __call__(self, ins):
        self.n += 1
        ins.then_inc(self.sem, 1)
        self.eng.wait_ge(self.sem, self.base + self.n)


class Kit:

    def sem(self, name):
        self.sems.append(self.nc.alloc_semaphore(name=name))
        return self.sems[-1]

    def recycle(self):
        nums = sorted(s.num for s in self.sems)
        runs = [[nums[0], nums[0]]]
        for n in nums[1:]:
            if n == runs[-1][1] + 1:
                runs[-1][1] = n
            else:
                runs.append([n, n])
        with self.nc.Block() as block:
            @block.gpsimd
            def _(pool):
                for lo, hi in runs:
                    pool.sem_clear(range(lo, hi + 1))
        for s in self.sems:
            self.nc.release_semaphore(s)
        self.sems = []


def rows_of(dram):
    return dram.rearrange("(t p) d -> p t d", p=PT)


def chunks_of(dram):
    return dram.rearrange("(k p) n -> p k n", p=128)


def spread(dram, n):
    return dram.rearrange("(a n) -> a n", a=1).to_broadcast([PT, n])


def setup(nc, k, a):
    zeroed, made, loaded = k.sem("zeroed"), k.sem("made"), k.sem("x_loaded")
    with nc.Block() as block:
        @block.sync
        def _(sp):
            sp.dma_start(k.X[:], rows_of(a["x"])).then_inc(loaded, 16)
            sp.wait_ge(loaded, 16)

        @block.gpsimd
        def _(pool):
            pool.memset(k.ident[:], 0.0).then_inc(zeroed, 1)
            pool.memset(k.ones[:], 1.0).then_inc(made, 1)
            pool.memset(k.sel[:], 0.0).then_inc(zeroed, 1)
            pool.wait_ge(zeroed, 2)
            pool.affine_select(out=k.ident[:], in_=k.ident[:], compare_op=ALU.not_equal, fill=1.0, base=0,
                               pattern=[[-1, 128]], channel_multiplier=1).then_inc(made, 1)
            pool.affine_select(out=k.sel[:], in_=k.sel[:], compare_op=ALU.not_equal, fill=1.0, base=0,
                               pattern=[[-1, 8], [0, PT]], channel_multiplier=1).then_inc(made, 1)
            pool.iota(k.iota8[:], pattern=[[1, 8]], base=0, channel_multiplier=0,
                      allow_small_or_imprecise_dtypes=True).then_inc(made, 1)
            pool.wait_ge(made, 4)


def layernorm(nc, k, name, src, dst, gain=None, shift=None, spare=None):
    stats, aggregated, deviation, inverse = (k.sem(f"{name}_{s}") for s in ("stats", "aggr", "std", "rstd"))
    normal, turned, stored, steps, loaded = (k.sem(f"{name}_{s}") for s in ("normal", "turned", "stored", "steps", "affine"))
    spared = k.sem(f"{name}_spared")
    with ExitStack() as ctx:
        st = ctx.enter_context(nc.sbuf_tensor(f"{name}_st", [PT, NT, 2, 6], F32))
        mv = ctx.enter_context(nc.sbuf_tensor(f"{name}_mv", [PT, NT, 2], F32))
        std = ctx.enter_context(nc.sbuf_tensor(f"{name}_sd", [PT, NT], F32))
        rstd = ctx.enter_context(nc.sbuf_tensor(f"{name}_rs", [PT, NT], F32))
        gb = ctx.enter_context(nc.sbuf_tensor(f"{name}_gb", [PT, 2, D], F32)) if gain is not None else None
        with nc.Block() as block:
            if gain is not None:
                @block.sync
                def _(sp):
                    sp.dma_start(gb[:, 0, :], spread(gain, D)).then_inc(loaded, 16)
                    sp.dma_start(gb[:, 1, :], spread(shift, D)).then_inc(loaded, 16)
                    sp.wait_ge(loaded, 32)

            @block.vector
            def _(dve):
                with dve.Fori(0, NT) as t:
                    for h in range(2):
                        dve.bn_stats(st[:, t, h, :], src[:, t, h * HALF:(h + 1) * HALF]).then_inc(stats, 1)
                dve.wait_ge(stats, 2 * NT)
                for t in range(NT):
                    dve.bn_aggr(mv[:, t, :], st[:, t, :, :]).then_inc(aggregated, 1)
                dve.wait_ge(deviation, 1)
                dve.reciprocal(rstd[:], std[:]).then_inc(inverse, 1)
                dve.wait_ge(inverse, 1)
                if gain is not None:
                    dve.wait_ge(loaded, 32)
                for t in range(NT):
                    link = Chain(dve, steps, 2 * t)
                    last = dve.tensor_scalar(dst[:, t, :], src[:, t, :], mv[:, t, 0:1], rstd[:, t:t + 1],
                                             ALU.subtract, ALU.mult)
                    if gain is not None:
                        link(last)
                        link(dve.tensor_tensor(dst[:, t, :], dst[:, t, :], gb[:, 0, :], ALU.mult))
                        last = dve.tensor_tensor(dst[:, t, :], dst[:, t, :], gb[:, 1, :], ALU.add)
                    last.then_inc(normal, 1)

            @block.scalar
            def _(act):
                act.wait_ge(aggregated, NT)
                act.activation(std[:].rearrange("p (t o) -> p t o", o=1), mv[:, :, 1:2], ACT.Sqrt,
                               bias=k.ln_eps[0:PT, :]).then_inc(deviation, 1)
                for t in range(NT):
                    act.wait_ge(turned, t + 1)
                    act.activation(k.FT[:, :, t * PT:(t + 1) * PT].rearrange("p (a b) n -> p a b n", a=2),
                                   k.PS[:, 2 * (t % 2):2 * (t % 2) + 2, 0:3 * PT].rearrange("p a (b n) -> p a b n", b=3),
                                   ACT.Copy).then_inc(stored, 1)

            if spare is not None:
                @block.gpsimd
                def _(pool):
                    pool.memset(spare[:, :, :, DH0:DH0 + 1], 1.0).then_inc(spared, 1)
                    for t in range(NT):
                        pool.wait_ge(normal, t + 1)
                        pool.tensor_copy(spare[:, t, :, 0:DH0],
                                         dst[:, t, :].rearrange("p (h d) -> p h d", d=DH0)).then_inc(spared, 1)

            @block.tensor
            def _(pe):
                for t in range(NT):
                    pe.wait_ge(normal, t + 1)
                    if t >= 2:
                        pe.wait_ge(stored, t - 1)
                    for c in range(KD):
                        mm = pe.transpose(k.PS[:, 2 * (t % 2) + c // 3, (c % 3) * PT:(c % 3 + 1) * PT],
                                          dst[:, t, c * 128:(c + 1) * 128], k.ident[0:PT, 0:PT])
                    mm.then_inc(turned, 1)


def turn(nc, k, name, src, dst, chunks):
    turned, stored = k.sem(f"{name}_turned"), k.sem(f"{name}_stored")
    with nc.Block() as block:
        @block.tensor
        def _(pe):
            for t in range(NT):
                if t >= 2:
                    pe.wait_ge(stored, t - 1)
                for c in range(chunks):
                    mm = pe.transpose(k.PS[:, t % 2, c * PT:(c + 1) * PT], src[:, t, c * 128:(c + 1) * 128],
                                      k.ident[0:PT, 0:PT])
                mm.then_inc(turned, 1)

        @block.scalar
        def _(act):
            for t in range(NT):
                act.wait_ge(turned, t + 1)
                act.activation(dst[:, :, t * PT:(t + 1) * PT],
                               k.PS[:, t % 2, 0:chunks * PT].rearrange("p (c n) -> p c n", c=chunks),
                               ACT.Copy).then_inc(stored, 1)


def rows_product(pe, k, lhs, rhs, chunks, width, ready, freed, base=0):
    for t in range(NT):
        if t >= 2:
            pe.wait_ge(freed, base + t - 1)
        for h in range(2):
            for c in range(chunks):
                mm = pe.matmul(k.PS[0:PT, 2 * (t % 2) + h, 0:width // 2], lhs[:, c, t * PT:(t + 1) * PT],
                               rhs[:, c, h * (width // 2):(h + 1) * (width // 2)],
                               start=(c == 0), stop=(c == chunks - 1))
        mm.then_inc(ready, 1)


def pair_bank(k, t, width=D):
    return k.PS[0:PT, 2 * (t % 2):2 * (t % 2) + 2, 0:width // 2]


def halves(ap):
    return ap.rearrange("p (a n) -> p a n", a=2)


def count_edges(nc, k, a):
    loaded, cast, iotas, hot, counted, stored, diag = (
        k.sem(f"count_{s}") for s in ("loaded", "cast", "iota", "hot", "counted", "stored", "diag"))
    T2 = 2 * PT
    with ExitStack() as ctx:
        raw = ctx.enter_context(nc.sbuf_tensor("edges_raw", [PT, 2, EC], I32))
        ends = ctx.enter_context(nc.sbuf_tensor("edges", [PT, 2, EC], F32))
        iota = ctx.enter_context(nc.sbuf_tensor("iota_nodes", [PT, N], F16))
        hd = ctx.enter_context(nc.sbuf_tensor("dst_hot", [PT, 4, N], BF16))
        hs = ctx.enter_context(nc.sbuf_tensor("src_hot", [PT, 4, T2], BF16))
        with nc.Block() as block:
            @block.sync
            def _(sp):
                sp.dma_start(raw[:, 0, :], a["src"].rearrange("(p c) -> p c", c=EC)).then_inc(loaded, 16)
                sp.dma_start(raw[:, 1, :], a["dst"].rearrange("(p c) -> p c", c=EC)).then_inc(loaded, 16)
                sp.wait_ge(loaded, 32)

            @block.gpsimd
            def _(pool):
                pool.iota(iota[:], pattern=[[1, N]], base=0, channel_multiplier=0,
                          allow_small_or_imprecise_dtypes=True).then_inc(iotas, 1)

            @block.vector
            def _(dve):
                dve.wait_ge(loaded, 32)
                dve.tensor_copy(ends[:], raw[:]).then_inc(cast, 1)
                dve.wait_ge(cast, 1)
                dve.wait_ge(iotas, 1)

                def block_of(done, c, s, lo):
                    dve.tensor_scalar(hd[:, s, :], iota[:], ends[:, 1, bass.ds(c, 1)], None, ALU.is_equal).then_inc(hot, 1)
                    dve.tensor_scalar(hs[:, s, :], iota[:, lo:lo + T2], ends[:, 0, bass.ds(c, 1)], None,
                                      ALU.is_equal).then_inc(hot, 1)

                for pair in range(NT // 2):
                    with dve.Fori(0, EC // 4) as quad:
                        c = 4 * quad
                        for s in range(4):
                            if pair == 0:
                                dve.wait_ge(counted, c + s + 1)
                            else:
                                dve.wait_ge(counted, c + s + 1 + EC * pair)
                            block_of(None, c + s, s, pair * T2)

            @block.tensor
            def _(pe):
                for s in range(4):
                    pe.matmul(k.PS[0:1, 7, 0:64], k.ident[0:128, 0:1], k.ident[0:128, 0:64],
                              start=True, stop=True).then_inc(counted, 1)
                for pair in range(NT // 2):
                    if pair:
                        pe.wait_ge(stored, pair)

                    def block_of(c, s, start, stop):
                        pe.wait_ge(hot, 2 * (c + s + 1 + EC * pair))
                        for j in range(2):
                            for b, (lo, n) in enumerate(CHUNKS):
                                mm = pe.matmul(k.PS[0:PT, 3 * j + b, 0:n], hs[:, s, j * PT:(j + 1) * PT],
                                               hd[:, s, lo:lo + n], start=start, stop=stop, skip_group_check=True)
                        mm.then_inc(counted, 1)

                    for s in range(4):
                        block_of(0, s, s == 0, False)
                    with pe.Fori(1, EC // 4) as quad:
                        c = 4 * quad
                        for s in range(4):
                            block_of(c, s, False, False)

            @block.scalar
            def _(act):
                for pair in range(NT // 2):
                    act.wait_ge(counted, 4 + EC * (pair + 1))
                    for j in range(2):
                        for b, (lo, n) in enumerate(CHUNKS):
                            ins = act.activation(k.CT[:, 2 * pair + j, lo:lo + n], k.PS[0:PT, 3 * j + b, 0:n], ACT.Copy)
                            ins.then_inc(diag, 1)
                    act.wait_ge(diag, 6 * (pair + 1))
                    act.activation(k.scrap[0:1, 0:1], k.CT[0:1, 2 * pair, 0:1], ACT.Copy).then_inc(stored, 1)
        with nc.Block() as block:
            @block.vector
            def _(dve):
                for t in range(NT):
                    blk = k.CT[:, t, t * PT:(t + 1) * PT]
                    dve.tensor_tensor(blk, blk, k.ident[0:PT, 0:PT], ALU.add).then_inc(cast, 1)


def gcn(nc, k, a):
    loaded, degreed, rooted, inverted, made, scaled, summed, added, biased, biased2 = (
        k.sem(f"gcn_{s}") for s in ("loaded", "deg", "root", "dinv", "made", "scaled", "summed", "added", "biased", "bias"))
    with ExitStack() as ctx:
        W = ctx.enter_context(nc.sbuf_tensor("gcn_W", [128, KD, D], F32))
        hs = ctx.enter_context(nc.sbuf_tensor("gcn_h", [PT, NT, D], F32))
        bias = ctx.enter_context(nc.sbuf_tensor("gcn_b", [PT, D], F32))
        root = ctx.enter_context(nc.sbuf_tensor("gcn_root", [PT, NT], F32))
        dinv = ctx.enter_context(nc.sbuf_tensor("gcn_dinv", [PT, NT], F32))
        with nc.Block() as block:
            @block.sync
            def _(sp):
                sp.dma_start(W[:], chunks_of(a["L0_gnn_W"])).then_inc(loaded, 16)
                sp.dma_start(bias[:], spread(a["L0_gnn_b"], D)).then_inc(loaded, 16)
                sp.wait_ge(loaded, 32)

            @block.tensor
            def _(pe):
                for d in range(NT):
                    for s in range(NT):
                        mm = pe.matmul(k.PS[0:PT, 7, d:d + 1], k.CT[:, s, d * PT:(d + 1) * PT], k.ones[0:PT, 0:1],
                                       start=(s == 0), stop=(s == NT - 1))
                mm.then_inc(degreed, 1)
                pe.wait_ge(loaded, 32)
                rows_product(pe, k, k.FT, W, KD, D, made, scaled)
                pe.wait_ge(scaled, NT)
                for d in range(NT):
                    if d >= 2:
                        pe.wait_ge(added, d - 1)
                    for h in range(2):
                        for s in range(NT):
                            mm = pe.matmul(k.PS[0:PT, 2 * (d % 2) + h, 0:HALF], k.CT[:, s, d * PT:(d + 1) * PT],
                                           hs[:, s, h * HALF:(h + 1) * HALF], start=(s == 0), stop=(s == NT - 1))
                    mm.then_inc(summed, 1)

            @block.scalar
            def _(act):
                act.wait_ge(degreed, 1)
                act.activation(root[:], k.PS[0:PT, 7, 0:NT], ACT.Sqrt).then_inc(rooted, 1)
                act.wait_ge(inverted, 1)
                for t in range(NT):
                    act.wait_ge(made, t + 1)
                    act.activation(halves(hs[:, t, :]), pair_bank(k, t), ACT.Copy,
                                   scale=dinv[:, t:t + 1]).then_inc(scaled, 1)

            @block.vector
            def _(dve):
                dve.wait_ge(rooted, 1)
                dve.reciprocal(dinv[:], root[:]).then_inc(inverted, 1)
                dve.wait_ge(inverted, 1)
                for t in range(NT):
                    dve.wait_ge(biased, t + 1)
                    dve.wait_ge(summed, t + 1)
                    dve.scalar_tensor_tensor(out=halves(k.X[:, t, :]), in0=pair_bank(k, t), scalar=dinv[:, t:t + 1],
                                             in1=halves(k.X[:, t, :]), op0=ALU.mult, op1=ALU.add).then_inc(added, 1)

            @block.gpsimd
            def _(pool):
                pool.wait_ge(loaded, 32)
                for t in range(NT):
                    pool.tensor_tensor(k.X[:, t, :], k.X[:, t, :], bias[:], ALU.add).then_inc(biased, 1)


def favor(nc, k, a):
    names = ("loaded", "copied", "u", "max", "bias", "peak", "peakT", "top", "spread", "shift", "decay", "q", "kp",
             "turned", "qt", "ctx", "cx", "num", "rden", "tmp", "added", "proj", "projT", "sq", "free")
    s = {n: k.sem(f"fav_{n}") for n in names}
    SC = SC0
    with ExitStack() as ctx:
        sb = lambda n, sh: ctx.enter_context(nc.sbuf_tensor(n, sh, F32))
        HV, htp, prow, proj = k.HV, sb("fav_htp", [128, N]), sb("fav_prow", [128, 2, DH0]), sb("fav_proj", [128, M0])
        QE, KP, QT = sb("fav_QE", [PT, NT, M0]), sb("fav_KP", [PT, NT, M0]), sb("fav_QT", [128, 2, N])
        CX, DG, sq = sb("fav_CX", [128, 2, DH0 + 1]), sb("fav_DG", [PT, NT, HEADS0]), sb("fav_sq", [PT, HEADS0, DH0])
        RM, NB, SK, pk, g1, NK = (sb("fav_RM", [PT, NT]), sb("fav_NB", [PT, NT]), sb("fav_SK", [PT, NT]),
                                  sb("fav_pk", [PT, 1]), sb("fav_g1", [1, 1]), sb("fav_NK", [PT, 1]))
        RD, TM = sb("fav_RD", [PT, NT]), sb("fav_TM", [PT, NT, DH0])
        U = k.PS[0:PT, 0:5, :].rearrange("p b (c m) -> p (b c) m", c=2)
        NUM = k.PS[0:PT, 0:2, 0:5 * (DH0 + 1)].rearrange("p b (c m) -> p b c m", c=5)
        CTX = k.PS[:, 7, 256:256 + 2 * (DH0 + 1)].rearrange("p (m d) -> p m d", m=2)
        with nc.Block() as block:
            @block.sync
            def _(sp):
                pv = a["L0_mix_proj"].rearrange("(c p) d -> p c d", p=128)
                for j in range(2):
                    sp.dma_start(k.pdup[:, :, j, :], pv).then_inc(s["loaded"], 16)
                sp.wait_ge(s["loaded"], 32)

            @block.tensor
            def _(pe):
                pe.wait_ge(s["loaded"], 32)
                for c in range(2):
                    mm = pe.transpose(k.PS[:, 7, c * 128:(c + 1) * 128],
                                      k.pdup[:, c, :, :].rearrange("p a d -> p (a d)"), k.ident[:])
                mm.then_inc(s["proj"], 1)

            @block.vector
            def _(dve):
                dve.wait_ge(s["proj"], 1)
                dve.tensor_copy(proj[:], k.PS[:, 7, 0:256]).then_inc(s["projT"], 1)
                for t in range(NT):
                    link = Chain(dve, s["sq"], 2 * t)
                    link(dve.tensor_tensor(sq[:], HV[:, t, :, 0:DH0], HV[:, t, :, 0:DH0], ALU.mult))
                    link(dve.tensor_reduce(DG[:, t, :], sq[:], AX.X, ALU.add))
                dve.tensor_scalar(DG[:], DG[:], 0.5 * SC * SC, None, ALU.mult).then_inc(s["sq"], 1)
        with nc.Block() as block:
            @block.gpsimd
            def _(pool):
                with pool.Fori(0, HEADS0 // 2) as pr:
                    pool.wait_ge(s["free"], pr + 1)
                    pool.tensor_copy(htp[:], k.FT[:, pr, :]).then_inc(s["copied"], 1)

            @block.tensor
            def _(pe):
                pe.matmul(k.PS[0:1, 7, 0:64], k.ident[:, 0:1], k.ident[:, 0:64],
                          start=True, stop=True).then_inc(s["free"], 1)
                with pe.Fori(0, HEADS0 // 2) as pr:
                    pe.wait_ge(s["copied"], pr + 1)
                    for j in range(2):
                        h = 2 * pr + j
                        lo = DH0 * j
                        pe.wait_ge(s["added"], h + 1)
                        for t in range(NT):
                            mm = pe.matmul(U[:, t, :], htp[lo:lo + DH0, t * PT:(t + 1) * PT], proj[lo:lo + DH0, :],
                                           start=True, stop=True)
                        mm.then_inc(s["u"], 1)
                        if j == 1:
                            pass
                        pe.wait_ge(s["peak"], h + 1)
                        pe.transpose(k.PS[0:1, 7, 0:PT], pk[:], k.ident[0:PT, 0:PT]).then_inc(s["peakT"], 1)
                        pe.wait_ge(s["top"], h + 1)
                        pe.matmul(k.PS[0:PT, 7, 128:129], k.ones[0:1, 0:PT], g1[:], start=True, stop=True)\
                            .then_inc(s["spread"], 1)
                        pe.wait_ge(s["q"], h + 1)
                        for g in range(NT // 2):
                            if g >= 2:
                                pe.wait_ge(s["qt"], 5 * h + g - 1)
                            for m in range(2):
                                for i in range(2):
                                    mm = pe.transpose(k.PS[:, 5 + g % 2, (2 * m + i) * PT:(2 * m + i + 1) * PT],
                                                      QE[:, 2 * g + i, m * 128:(m + 1) * 128], k.ident[0:PT, 0:PT])
                            mm.then_inc(s["turned"], 1)
                        pe.wait_ge(s["kp"], h + 1)
                        for m in range(2):
                            for t in range(NT):
                                mm = pe.matmul(CTX[:, m, :], KP[:, t, m * 128:(m + 1) * 128],
                                               HV[:, t, bass.ds(h, 1), :].rearrange("p o d -> p (o d)"),
                                               start=(t == 0), stop=(t == NT - 1))
                        mm.then_inc(s["ctx"], 1)
                        pe.wait_ge(s["cx"], h + 1)
                        pe.wait_ge(s["qt"], 5 * h + 5)
                        for t in range(NT):
                            for m in range(2):
                                mm = pe.matmul(NUM[:, t // 5, t % 5, :], QT[:, m, t * PT:(t + 1) * PT], CX[:, m, :],
                                               start=(m == 0), stop=(m == 1))
                        mm.then_inc(s["num"], 1)
                    pe.matmul(k.PS[0:1, 7, 0:64], k.ident[:, 0:1], k.ident[:, 0:64],
                              start=True, stop=True).then_inc(s["free"], 1)

            @block.scalar
            def _(act):
                act.preload_act_table(ACT.Exp)
                with act.Fori(0, HEADS0) as h:
                    act.wait_ge(s["bias"], h + 1)
                    for t in range(NT):
                        ins = act.activation(QE[:, t, :], U[:, t, :], ACT.Exp, scale=SC, bias=NB[:, t:t + 1])
                    ins.then_inc(s["q"], 1)
                    act.wait_ge(s["shift"], h + 1)
                    act.activation(SK[:], RM[:], ACT.Exp, scale=SC, bias=NK[:]).then_inc(s["decay"], 1)
                    act.wait_ge(s["ctx"], h + 1)
                    act.activation(CX[:], CTX, ACT.Copy).then_inc(s["cx"], 1)

            @block.vector
            def _(dve):
                dve.memset(k.scrap[0:1, 0:1], 0.0).then_inc(s["added"], 1)
                with dve.Fori(0, HEADS0) as h:
                    dve.wait_ge(s["u"], h + 1)
                    dve.tensor_reduce(RM[:], U, AX.X, ALU.max).then_inc(s["max"], 1)
                    dve.wait_ge(s["max"], h + 1)
                    dve.reduce_max(pk[:], RM[:], AX.X).then_inc(s["peak"], 1)
                    dve.scalar_tensor_tensor(out=NB[:].rearrange("p (t o) -> p t o", o=1),
                                             in0=RM[:].rearrange("p (t o) -> p t o", o=1), scalar=-SC,
                                             in1=DG[:, :, bass.ds(h, 1)], op0=ALU.mult, op1=ALU.subtract)\
                        .then_inc(s["bias"], 1)
                    dve.wait_ge(s["peakT"], h + 1)
                    dve.reduce_max(g1[:], k.PS[0:1, 7, 0:PT], AX.X).then_inc(s["top"], 1)
                    dve.wait_ge(s["spread"], h + 1)
                    dve.tensor_scalar(NK[:], k.PS[0:PT, 7, 128:129], -SC, None, ALU.mult).then_inc(s["shift"], 1)
                    dve.wait_ge(s["decay"], h + 1)
                    dve.wait_ge(s["q"], h + 1)
                    for t in range(NT):
                        ins = dve.tensor_scalar(KP[:, t, :], QE[:, t, :], SK[:, t:t + 1], EPS0, ALU.mult, ALU.add)
                    ins.then_inc(s["kp"], 1)
                    for g in range(NT // 2):
                        dve.wait_ge(s["turned"], 5 * h + g + 1)
                        dve.tensor_scalar(QT[:, :, 2 * g * PT:(2 * g + 2) * PT],
                                          k.PS[:, 5 + g % 2, 0:4 * PT].rearrange("p (m n) -> p m n", m=2),
                                          EPS0, None, ALU.add).then_inc(s["qt"], 1)
                    dve.wait_ge(s["num"], h + 1)
                    dve.reciprocal(RD[:].rearrange("p (b c o) -> p b c o", b=2, o=1), NUM[:, :, :, DH0:DH0 + 1])\
                        .then_inc(s["rden"], 1)
                    dve.wait_ge(s["rden"], h + 1)
                    dve.tensor_tensor(TM[:].rearrange("p (b c) d -> p b c d", b=2), NUM[:, :, :, 0:DH0],
                                      RD[:].rearrange("p (b c o) -> p b c o", b=2, o=1).to_broadcast([PT, 2, 5, DH0]),
                                      ALU.mult).then_inc(s["tmp"], 1)
                    dve.wait_ge(s["tmp"], h + 1)
                    xs = k.XN[:, :, bass.ds(h * DH0, DH0)]
                    dve.tensor_tensor(xs, xs, TM[:], ALU.add).then_inc(s["added"], 1)


def cols_product(pe, k, w, src, chunks, outs, ready, freed, base=0):
    i = 0
    for f in range(outs):
        for lo, n in CHUNKS:
            if isinstance(base, int) and base == 0 and i < 2:
                pass
            else:
                pe.wait_ge(freed, base + i - 1)
            for c in range(chunks):
                mm = pe.matmul(k.PS[:, 4 + i % 2, 0:n], w[:, c, f * 128:(f + 1) * 128], src[:, c, lo:lo + n],
                               start=(c == 0), stop=(c == chunks - 1))
            mm.then_inc(ready, 1)
            i += 1


def mlp(nc, k, name, w1, b1, func, w2, b2, src, chunks, hidden, extra=None):
    loaded, made, stored, out, added, steps = (
        k.sem(f"{name}_{s}") for s in ("loaded", "hidden", "stored", "out", "added", "steps"))
    outs = hidden // 128
    with ExitStack() as ctx:
        A = ctx.enter_context(nc.sbuf_tensor(f"{name}_w1", [128, chunks, hidden], F32))
        B = ctx.enter_context(nc.sbuf_tensor(f"{name}_w2", [128, outs, D], F32))
        ba = ctx.enter_context(nc.sbuf_tensor(f"{name}_b1", [128, outs], F32))
        bb = ctx.enter_context(nc.sbuf_tensor(f"{name}_b2", [PT, D], F32))
        G = ctx.enter_context(nc.sbuf_tensor(f"{name}_h", [128, outs, N], F32))
        with nc.Block() as block:
            @block.sync
            def _(sp):
                sp.dma_start(A[:], chunks_of(w1)).then_inc(loaded, 16)
                sp.dma_start(B[:], chunks_of(w2)).then_inc(loaded, 16)
                with nc.allow_non_contiguous_dma(reason="one bias value per partition"):
                    sp.dma_start(ba[:], b1.rearrange("(k p) -> p k", p=128)).then_inc(loaded, 16)
                sp.dma_start(bb[:], spread(b2, D)).then_inc(loaded, 16)
                sp.wait_ge(loaded, 64)

            @block.tensor
            def _(pe):
                pe.wait_ge(loaded, 64)
                cols_product(pe, k, A, src, chunks, outs, made, stored)
                pe.wait_ge(stored, 3 * outs)
                rows_product(pe, k, G, B, outs, D, out, added)

            @block.scalar
            def _(act):
                act.wait_ge(loaded, 64)
                i = 0
                for f in range(outs):
                    for lo, n in CHUNKS:
                        act.wait_ge(made, i + 1)
                        act.activation(G[:, f, lo:lo + n], k.PS[:, 4 + i % 2, 0:n], func,
                                       bias=ba[:, f:f + 1]).then_inc(stored, 1)
                        i += 1

            @block.vector
            def _(dve):
                dve.wait_ge(loaded, 64)
                per = 2 + (extra is not None)
                link = Chain(dve, steps)
                for t in range(NT):
                    dve.wait_ge(out, t + 1)
                    ins = dve.tensor_tensor(halves(k.X[:, t, :]), pair_bank(k, t), halves(k.X[:, t, :]), ALU.add)
                    ins.then_inc(added, 1)
                    dve.wait_ge(added, t + 1)
                    link(dve.tensor_tensor(k.X[:, t, :], k.X[:, t, :], bb[:], ALU.add))
                    if extra is not None:
                        link(dve.tensor_tensor(k.X[:, t, :], k.X[:, t, :], extra[:, t, :], ALU.add))


def router(nc, k, name, gate, gate_bias, experts, top, b_proj, transposed):
    loaded, turned, gateT, scored, logits, steps, combT, comb_out, biased, expd, ct = (
        k.sem(f"{name}_{s}") for s in ("loaded", "turned", "gateT", "scored", "logits", "steps", "combT", "out",
                                        "biased", "exp", "ct"))
    with ExitStack() as ctx:
        sb = lambda n, sh, d=F32: ctx.enter_context(nc.sbuf_tensor(f"{name}_{n}", sh, d))
        gr, G = sb("gr", [experts, D]), sb("G", [128, KD, experts])
        LG, M8, I8, IF = sb("LG", [PT, NT, 8]), sb("M8", [PT, NT, 8]), sb("I8", [PT, NT, 8], U32), sb("IF", [PT, NT, 8])
        bg, bp = sb("bg", [PT, experts]), sb("bp", [experts, D])
        dl, w0, w1, c1, CB = sb("dl", [PT, NT]), sb("w0", [PT, NT]), sb("w1", [PT, NT]), sb("c1", [PT, NT, 8]), sb("CB", [8, N])
        with nc.Block() as block:
            @block.sync
            def _(sp):
                if transposed:
                    sp.dma_start(gr[:], gate).then_inc(loaded, 16)
                else:
                    sp.dma_start(G[:], chunks_of(gate)).then_inc(loaded, 16)
                if gate_bias is not None:
                    sp.dma_start(bg[:], spread(gate_bias, experts)).then_inc(loaded, 16)
                else:
                    sp.dma_start(bg[:, 0:1], spread(b_proj[0, 0:1], 1)).then_inc(loaded, 16)
                sp.dma_start(bp[:], b_proj).then_inc(loaded, 16)
                sp.wait_ge(loaded, 48)

            @block.tensor
            def _(pe):
                pe.wait_ge(loaded, 48)
                if transposed:
                    for c in range(KD):
                        mm = pe.transpose(k.PS[:, 7, c * experts:(c + 1) * experts], gr[:, c * 128:(c + 1) * 128],
                                          k.ident[0:experts, 0:experts])
                    mm.then_inc(turned, 1)
                    pe.wait_ge(gateT, 1)
                for t in range(NT):
                    for c in range(KD):
                        mm = pe.matmul(k.PS[0:PT, 6, t * 8:t * 8 + experts], k.FT[:, c, t * PT:(t + 1) * PT],
                                       G[:, c, :], start=(c == 0), stop=(c == KD - 1))
                mm.then_inc(scored, 1)
                pe.wait_ge(steps, 100)
                for t in range(NT):
                    mm = pe.transpose(k.PS[0:8, t // 4, (t % 4) * PT:(t % 4 + 1) * PT], k.comb[:, t, :],
                                      k.ident[0:PT, 0:PT])
                mm.then_inc(combT, 1)
                pe.wait_ge(ct, 1)
                for t in range(NT):
                    if t >= 2:
                        pe.wait_ge(biased, t - 1)
                    for h in range(2):
                        mm = pe.matmul(k.PS[0:PT, 2 * (t % 2) + h, 0:HALF], CB[0:experts, t * PT:(t + 1) * PT],
                                       bp[:, h * HALF:(h + 1) * HALF], start=True, stop=True)
                    mm.then_inc(comb_out, 1)

            @block.scalar
            def _(act):
                if top == 2:
                    act.wait_ge(logits, 2)
                    act.activation(w1[:], dl[:], ACT.Exp).then_inc(expd, 1)

            @block.vector
            def _(dve):
                dve.wait_ge(loaded, 48)
                link = Chain(dve, steps)
                if transposed:
                    dve.wait_ge(turned, 1)
                    dve.tensor_copy(G[:], k.PS[:, 7, 0:KD * experts].rearrange("p (c e) -> p c e", c=KD))\
                        .then_inc(gateT, 1)
                link(dve.memset(LG[:], -3.0e38))
                dve.wait_ge(scored, 1)
                ps = k.PS[0:PT, 6, 0:8 * NT].rearrange("p (t e) -> p t e", e=8)[:, :, 0:experts]
                if gate_bias is not None:
                    link(dve.tensor_tensor(LG[:, :, 0:experts], ps,
                                           bg[:].rearrange("p (o e) -> p o e", o=1).to_broadcast([PT, NT, experts]), ALU.add))
                else:
                    link(dve.tensor_copy(LG[:, :, 0:experts], ps))
                for t in range(NT):
                    link(dve.max(M8[:, t, :], LG[:, t, :]))
                    link(dve.max_index(I8[:, t, :], M8[:, t, :], LG[:, t, :]))
                link(dve.tensor_copy(IF[:], I8[:]))
                iota = k.iota8[:].rearrange("p (o e) -> p o e", o=1).to_broadcast([PT, NT, 8])
                col = lambda ap: ap.rearrange("p (t o) -> p t o", o=1)
                wide = lambda ap: col(ap).to_broadcast([PT, NT, 8])
                link(dve.tensor_tensor(k.comb[:], iota, IF[:, :, 0:1].to_broadcast([PT, NT, 8]), ALU.is_equal))
                if top == 2:
                    dve.tensor_tensor(col(dl[:]), M8[:, :, 1:2], M8[:, :, 0:1], ALU.subtract).then_inc(logits, 2)
                    dve.wait_ge(expd, 1)
                    link(dve.tensor_scalar(w0[:], w1[:], 1.0, None, ALU.add))
                    link(dve.reciprocal(w0[:], w0[:]))
                    link(dve.tensor_tensor(w1[:], w1[:], w0[:], ALU.mult))
                    link(dve.tensor_tensor(c1[:], iota, IF[:, :, 1:2].to_broadcast([PT, NT, 8]), ALU.is_equal))
                    link(dve.tensor_tensor(c1[:], c1[:], wide(w1[:]), ALU.mult))
                    link(dve.tensor_tensor(k.comb[:], k.comb[:], wide(w0[:]), ALU.mult))
                    link(dve.tensor_tensor(k.comb[:], k.comb[:], c1[:], ALU.add))
                dve.nop().then_inc(steps, 100 - link.n)
                dve.wait_ge(combT, 1)
                for b, (lo, n) in enumerate(CHUNKS):
                    ins = dve.tensor_copy(CB[:, lo:lo + n], k.PS[0:8, b, 0:n])
                ins.then_inc(ct, 1)
                for t in range(NT):
                    dve.wait_ge(comb_out, t + 1)
                    dve.tensor_tensor(halves(k.X[:, t, :]), pair_bank(k, t), halves(k.X[:, t, :]), ALU.add)\
                        .then_inc(biased, 1)


def experts_mlp(nc, k, name, w1, b1, w2, experts):
    loaded = [k.sem(f"{name}_loaded{s}") for s in range(2)]
    made, stored, out, added = (k.sem(f"{name}_{s}") for s in ("hidden", "stored", "out", "added"))
    P1 = 3 * KF
    with ExitStack() as ctx:
        sb = lambda n, sh: ctx.enter_context(nc.sbuf_tensor(f"{name}_{n}", sh, F32))
        A = [sb(f"w1_{s}", [128, KD, F0]) for s in range(2)]
        B = [sb(f"w2_{s}", [128, KF, D]) for s in range(2)]
        ba = [sb(f"b1_{s}", [128, KF]) for s in range(2)]
        G = sb("h", [128, KF, N])
        with nc.Block() as block:
            @block.sync
            def _(sp):
                def load(e, s):
                    sp.dma_start(A[s][:], w1[bass.ds(e, 1), :, :].rearrange("o (k p) n -> p (o k) n", p=128))\
                        .then_inc(loaded[s], 16)
                    sp.dma_start(B[s][:], w2[bass.ds(e, 1), :, :].rearrange("o (k p) n -> p (o k) n", p=128))\
                        .then_inc(loaded[s], 16)
                    with nc.allow_non_contiguous_dma(reason="one bias value per partition"):
                        sp.dma_start(ba[s][:], b1[bass.ds(e, 1), :].rearrange("o (k p) -> p (o k)", p=128))\
                            .then_inc(loaded[s], 16)

                for s in range(2):
                    load(s, s)
                with sp.Fori(1, experts // 2) as couple:
                    for s in range(2):
                        e = 2 * couple + s
                        sp.wait_ge(out, NT * (e - 1))
                        load(e, s)
                for s in range(2):
                    sp.wait_ge(loaded[s], 48 * (experts // 2))

            @block.tensor
            def _(pe):
                def expert(couple, s, first):
                    e = 2 * couple + s
                    pe.wait_ge(loaded[s], 48 * couple + 48)
                    i = 0
                    for f in range(KF):
                        for lo, n in CHUNKS:
                            if not (first and i < 2):
                                pe.wait_ge(stored, P1 * e + (i - 1))
                            for c in range(KD):
                                mm = pe.matmul(k.PS[:, 4 + i % 2, 0:n], A[s][:, c, f * 128:(f + 1) * 128],
                                               k.FT[:, c, lo:lo + n], start=(c == 0), stop=(c == KD - 1))
                            mm.then_inc(made, 1)
                            i += 1
                    pe.wait_ge(stored, P1 * e + P1)
                    for t in range(NT):
                        if not (first and t < 2):
                            pe.wait_ge(added, NT * e + (t - 1))
                        for h in range(2):
                            for c in range(KF):
                                mm = pe.matmul(k.PS[0:PT, 2 * (t % 2) + h, 0:HALF], G[:, c, t * PT:(t + 1) * PT],
                                               B[s][:, c, h * HALF:(h + 1) * HALF], start=(c == 0), stop=(c == KF - 1))
                        mm.then_inc(out, 1)

                for s in range(2):
                    expert(0, s, s == 0)
                with pe.Fori(1, experts // 2) as couple:
                    for s in range(2):
                        expert(couple, s, False)

            @block.scalar
            def _(act):
                act.preload_act_table(ACT.Gelu)

                def expert(couple, s, first):
                    e = 2 * couple + s
                    act.wait_ge(loaded[s], 48 * couple + 48)
                    if not first:
                        act.wait_ge(out, NT * e)
                    i = 0
                    for f in range(KF):
                        for lo, n in CHUNKS:
                            act.wait_ge(made, P1 * e + (i + 1))
                            act.activation(G[:, f, lo:lo + n], k.PS[:, 4 + i % 2, 0:n], ACT.Gelu,
                                           bias=ba[s][:, f:f + 1]).then_inc(stored, 1)
                            i += 1

                for s in range(2):
                    expert(0, s, s == 0)
                with act.Fori(1, experts // 2) as couple:
                    for s in range(2):
                        expert(couple, s, False)

            @block.vector
            def _(dve):
                with dve.Fori(0, experts) as e:
                    for t in range(NT):
                        dve.wait_ge(out, NT * e + (t + 1))
                        dve.scalar_tensor_tensor(out=halves(k.X[:, t, :]), in0=pair_bank(k, t),
                                                 scalar=k.comb[:, t, bass.ds(e, 1)],
                                                 in1=halves(k.X[:, t, :]), op0=ALU.mult, op1=ALU.add).then_inc(added, 1)


def mask(nc, k):
    turned, stored = k.sem("mask_turned"), k.sem("mask_stored")
    with nc.Block() as block:
        @block.tensor
        def _(pe):
            i = 0
            for d in range(NT):
                for g in range(0, NT, 4):
                    if i >= 2:
                        pe.wait_ge(stored, i - 1)
                    for s in range(g, min(g + 4, NT)):
                        mm = pe.transpose(k.PS[0:PT, i % 2, (s - g) * PT:(s - g + 1) * PT],
                                          k.CT[:, s, d * PT:(d + 1) * PT], k.ident[0:PT, 0:PT])
                    mm.then_inc(turned, 1)
                    i += 1

        @block.vector
        def _(dve):
            i = 0
            for d in range(NT):
                for lo, n in CHUNKS:
                    dve.wait_ge(turned, i + 1)
                    dve.tensor_scalar(k.MK[:, d, lo:lo + n], k.PS[0:PT, i % 2, 0:n], 0.5, NEG, ALU.is_lt, ALU.mult)\
                        .then_inc(stored, 1)
                    i += 1


def features(nc, k, name, src, chunks, w, hx, heads, width):
    loaded, made, stored, one = (k.sem(f"{name}_{s}") for s in ("loaded", "made", "stored", "one"))
    with ExitStack() as ctx:
        W = ctx.enter_context(nc.sbuf_tensor(f"{name}_W", [128, chunks, HID], F32))
        with nc.Block() as block:
            @block.sync
            def _(sp):
                sp.dma_start(W[:], chunks_of(w)).then_inc(loaded, 16)
                sp.wait_ge(loaded, 16)

            @block.gpsimd
            def _(pool):
                pool.memset(hx[:, :, :, width:width + 1], 1.0).then_inc(one, 1)

            @block.tensor
            def _(pe):
                pe.wait_ge(loaded, 16)
                for t in range(NT):
                    if t >= 2:
                        pe.wait_ge(stored, t - 1)
                    for c in range(chunks):
                        mm = pe.matmul(k.PS[0:PT, t % 2, 0:HID], src[:, c, t * PT:(t + 1) * PT], W[:, c, :],
                                       start=(c == 0), stop=(c == chunks - 1))
                    mm.then_inc(made, 1)

            @block.scalar
            def _(act):
                for t in range(NT):
                    act.wait_ge(made, t + 1)
                    act.activation(hx[:, t, :, 0:width], k.PS[0:PT, t % 2, 0:HID].rearrange("p (h d) -> p h d", h=heads),
                                   ACT.Copy).then_inc(stored, 1)


def gat(nc, k, name, a_src, a_dst, bias, hx, heads, width, dst):
    names = ("loaded", "steps", "rows", "rowsT", "spread", "spreadB", "maxed", "z", "brow", "browT", "b", "bB",
             "low", "lin", "e", "p", "sum", "out", "dd", "den")
    s = {n: k.sem(f"{name}_{n}") for n in names}
    parts = 1 if width * heads == HID and heads > 1 else 2
    span = N // parts
    W1 = width + 1
    per_bank = 5 if heads > 1 else 1
    banks = (NT // parts) // per_bank
    units = [(h, q) for h in range(heads) for q in range(parts)]
    with ExitStack() as ctx:
        sb = lambda n, sh, d=F32: ctx.enter_context(nc.sbuf_tensor(f"{name}_{n}", sh, d))
        av, bb = sb("av", [PT, 2, HID]), sb("bias", [PT, HID])
        tmp = sb("tmp", [PT, HID])
        AS, AD, MX, Z, LK = (sb(n, [PT, NT, heads]) for n in ("AS", "AD", "MX", "Z", "LK"))
        BB, AS2 = sb("BB", [PT, 2, NT, heads]), sb("AS2", [PT, NT, heads])
        spent = k.XN[:].rearrange("p t d -> p (t d)")[:, NT * HID:]
        low = spent[:, 0:2 * span].rearrange("p (s n) -> p s n", s=2)
        scrap, R = spent[:, 2 * N:3 * N], spent[0:8, 3 * N:4 * N]
        P = k.FT[0:PT, 2:5, 0:span]
        SB = sb("SB", [PT, 2, N])
        RD = sb("RD", [PT, NT])
        acc = lambda d: k.PS[0:PT, (d % (NT // parts)) // per_bank,
                             (d % per_bank) * W1:(d % per_bank + 1) * W1] if per_bank > 1 else \
            k.PS[0:PT, d % (NT // parts), 0:W1]
        with nc.Block() as block:
            @block.sync
            def _(sp):
                sp.dma_start(av[:, 0, :], a_src.rearrange("h d -> (h d)").rearrange("(a n) -> a n", a=1).to_broadcast([PT, HID])).then_inc(s["loaded"], 16)
                sp.dma_start(av[:, 1, :], a_dst.rearrange("h d -> (h d)").rearrange("(a n) -> a n", a=1).to_broadcast([PT, HID])).then_inc(s["loaded"], 16)
                sp.dma_start(bb[:], spread(bias, HID)).then_inc(s["loaded"], 16)
                sp.wait_ge(s["loaded"], 48)

            @block.vector
            def _(dve):
                link = Chain(dve, s["steps"])
                dve.wait_ge(s["loaded"], 48)
                hd = lambda ap: ap.rearrange("p (h d) -> p h d", h=heads)
                for t in range(NT):
                    for i, dest in enumerate((AS, AD)):
                        link(dve.tensor_tensor(hd(tmp[:]), hx[:, t, :, 0:width], hd(av[:, i, :]), ALU.mult))
                        link(dve.tensor_reduce(dest[:, t, :], hd(tmp[:]), AX.X, ALU.add))
                link(dve.tensor_scalar(AS2[:], AS[:], 0.2, None, ALU.mult))
                dve.nop().then_inc(s["rows"], 1)
                for b, (lo, n) in enumerate(CHUNKS):
                    if b == 0:
                        dve.wait_ge(s["rowsT"], 1)
                    ins = dve.tensor_copy(R[0:heads, lo:lo + n], k.PS[0:heads, b, 0:n])
                ins.then_inc(s["spread"], 1)
                for h in range(heads):
                    dve.wait_ge(s["spreadB"], h + 1)
                    for b, (lo, n) in enumerate(CHUNKS):
                        link(dve.tensor_copy(SB[:, 0, lo:lo + n], k.PS[0:PT, 3 + b, 0:n]))
                    for d in range(NT):
                        link(dve.tensor_tensor_reduce(scrap[:], k.MK[:, d, :], SB[:, 0, :], 1.0, -3.0e38,
                                                      ALU.add, ALU.max, MX[:, d, h:h + 1]))
                    dve.nop().then_inc(s["maxed"], 1)
                link(dve.tensor_tensor(Z[:], AD[:], MX[:], ALU.add))
                link(dve.tensor_scalar(LK[:], Z[:], 0.2, None, ALU.mult))
                link(dve.tensor_tensor(Z[:], Z[:], LK[:], ALU.max))
                link(dve.tensor_tensor(BB[:, 0], AD[:], Z[:], ALU.subtract))
                link(dve.scalar_tensor_tensor(out=BB[:, 1], in0=AD[:], scalar=0.2, in1=Z[:], op0=ALU.mult,
                                              op1=ALU.subtract))
                dve.nop().then_inc(s["z"], 1)

            @block.tensor
            def _(pe):
                pe.wait_ge(s["rows"], 1)
                for t in range(NT):
                    mm = pe.transpose(k.PS[0:heads, t // 4, (t % 4) * PT:(t % 4 + 1) * PT], AS[:, t, :],
                                      k.ident[0:PT, 0:PT])
                mm.then_inc(s["rowsT"], 1)
                pe.wait_ge(s["spread"], 1)
                for h in range(heads):
                    if h:
                        pe.wait_ge(s["maxed"], h)
                    for b, (lo, n) in enumerate(CHUNKS):
                        mm = pe.matmul(k.PS[0:PT, 3 + b, 0:n], k.sel[0:heads, h, :], R[0:heads, lo:lo + n],
                                       start=True, stop=True)
                    mm.then_inc(s["spreadB"], 1)
        R2 = sb("R2", [8, N])
        with nc.Block() as block:
            @block.tensor
            def _(pe):
                for i in range(2):
                    for t in range(NT):
                        mm = pe.transpose(k.PS[0:heads, 3 * i + t // 4, (t % 4) * PT:(t % 4 + 1) * PT],
                                          BB[:, i, t, :], k.ident[0:PT, 0:PT])
                mm.then_inc(s["browT"], 1)

            @block.vector
            def _(dve):
                dve.wait_ge(s["browT"], 1)
                for i, dest in enumerate((R, R2)):
                    for b, (lo, n) in enumerate(CHUNKS):
                        dve.tensor_copy(dest[0:heads, lo:lo + n], k.PS[0:heads, 3 * i + b, 0:n]).then_inc(s["brow"], 1)
        for u, (h, q) in enumerate(units):
            if q == 0:
                with nc.Block() as block:
                    @block.tensor
                    def _(pe):
                        for i, row in enumerate((R, R2)):
                            for b, (lo, n) in enumerate(CHUNKS):
                                mm = pe.matmul(k.PS[0:PT, 3 * i + b, 0:n], k.sel[0:heads, h, :], row[0:heads, lo:lo + n],
                                               start=True, stop=True)
                        mm.then_inc(s["b"], 1)

                    @block.vector
                    def _(dve):
                        dve.wait_ge(s["b"], h + 1)
                        for i in range(2):
                            for b, (lo, n) in enumerate(CHUNKS):
                                dve.tensor_copy(SB[:, i, lo:lo + n], k.PS[0:PT, 3 * i + b, 0:n]).then_inc(s["bB"], 1)
            with nc.Block() as block:
                lo = q * span
                tiles = range(q * (NT // parts), (q + 1) * (NT // parts))
                g0 = u * NT

                @block.scalar
                def _(act):
                    def lower(t):
                        if g0 + t >= 2:
                            act.wait_ge(s["lin"], g0 + t - 1)
                        act.activation(low[:, (g0 + t) % 2, :], SB[:, 1, lo:lo + span], ACT.Identity,
                                       bias=AS2[:, t, h:h + 1]).then_inc(s["low"], 1)
                    lower(0)
                    for t in range(NT):
                        if t + 1 < NT:
                            lower(t + 1)
                        act.wait_ge(s["lin"], g0 + t + 1)
                        act.activation(P[:, (g0 + t) % 3, :], P[:, (g0 + t) % 3, :], ACT.Exp).then_inc(s["e"], 1)

                @block.vector
                def _(dve):
                    def linear(t):
                        dve.wait_ge(s["low"], g0 + t + 1)
                        if g0 + t >= 3:
                            dve.wait_ge(s["sum"], g0 + t - 2)
                        dve.scalar_tensor_tensor(out=P[:, (g0 + t) % 3, :], in0=SB[:, 0, lo:lo + span],
                                                 scalar=AS[:, t, h:h + 1], in1=low[:, (g0 + t) % 2, :],
                                                 op0=ALU.add, op1=ALU.max).then_inc(s["lin"], 1)
                    linear(0)
                    for t in range(NT):
                        if t + 1 < NT:
                            linear(t + 1)
                        dve.wait_ge(s["e"], g0 + t + 1)
                        pt = P[:, (g0 + t) % 3, :]
                        dve.tensor_tensor(pt, pt, k.CT[:, t, lo:lo + span], ALU.mult).then_inc(s["p"], 1)
                    dve.wait_ge(s["sum"], g0 + NT)
                    nt = NT // parts
                    if per_bank > 1:
                        A = k.PS[0:PT, 0:banks, 0:per_bank * W1].rearrange("p b (c d) -> p b c d", d=W1)
                    else:
                        A = k.PS[0:PT, 0:banks, 0:W1].rearrange("p b (c d) -> p b c d", c=1)
                    rd = RD[:, 0:nt].rearrange("p (b c o) -> p b c o", b=banks, o=1)
                    link = Chain(dve, s["den"], 4 * u)
                    link(dve.tensor_scalar(rd, A[:, :, :, width:W1], 1e-16, None, ALU.add))
                    link(dve.reciprocal(rd, rd))
                    ov = dst[:, tiles[0]:tiles[-1] + 1, h * width:(h + 1) * width].rearrange(
                        "p (b c) d -> p b c d", b=banks)
                    link(dve.tensor_tensor(ov, A[:, :, :, 0:width], rd.to_broadcast([PT, banks, per_bank, width]), ALU.mult))
                    ov3 = dst[:, tiles[0]:tiles[-1] + 1, h * width:(h + 1) * width]
                    link(dve.tensor_tensor(ov3, ov3, bb[:, h * width:(h + 1) * width].rearrange("p (o d) -> p o d", o=1)
                                           .to_broadcast([PT, nt, width]), ALU.add))
                    dve.tensor_scalar(ov3, ov3, 0.0, None, ALU.max).then_inc(s["out"], 1)

                @block.tensor
                def _(pe):
                    for t in range(NT):
                        pe.wait_ge(s["p"], g0 + t + 1)
                        for i, d in enumerate(tiles):
                            mm = pe.matmul(acc(d), P[:, (g0 + t) % 3, i * PT:(i + 1) * PT],
                                           hx[:, t, h, :], start=(t == 0 and i % per_bank == 0), stop=(t == NT - 1),
                                           skip_group_check=True)
                        mm.then_inc(s["sum"], 1)


def linear_mixer(nc, k, a):
    names = ("wk", "wv", "wq", "wp", "ga", "k", "kf", "ks", "kr", "kst", "v", "vf", "kv", "kvt", "kvB", "q", "qf", "steps", "qs",
             "qr", "std", "n", "turned", "stored", "y", "added", "kvs")
    s = {n: k.sem(f"lin_{n}") for n in names}
    third = lambda i: chunks_of(a["L1_mix_w_qkv"])[:, :, i * D:(i + 1) * D]
    with ExitStack() as ctx:
        sb = lambda n, sh: ctx.enter_context(nc.sbuf_tensor(f"lin_{n}", sh, F32))
        W = sb("W", [128, KD, D])
        gb = sb("gb", [PT, 2, D])
        kv, kvB, sqj = sb("kv", [PT, 2, D]), sb("kvB", [PT, D]), sb("sqj", [PT, 2, HALF])
        ss, rn = sb("ss", [PT, NT]), sb("rn", [PT, NT])
        st, mv, sd, rs = sb("st", [PT, NT, 2, 6]), sb("mv", [PT, NT, 2]), sb("sd", [PT, NT]), sb("rs", [PT, NT])

        def norms(name, dst, save):
            with nc.Block() as block:
                @block.sync
                def _(sp):
                    sp.dma_start(W[:], third({"k": 1, "q": 0}[name])).then_inc(s["w" + name], 16)
                    sp.wait_ge(s["w" + name], 16)
                    if name == "q":
                        sp.dma_start(gb[:, 0, :], spread(a["L1_mix_ln_out_g"], D)).then_inc(s["ga"], 16)
                        sp.dma_start(gb[:, 1, :], spread(a["L1_mix_ln_out_b"], D)).then_inc(s["ga"], 16)
                        sp.wait_ge(s["ga"], 32)

                @block.tensor
                def _(pe):
                    pe.wait_ge(s["w" + name], 16)
                    rows_product(pe, k, k.FT, W, KD, D, s[name], s[name + "f"])

                @block.scalar
                def _(act):
                    for t in range(NT):
                        act.wait_ge(s[name], t + 1)
                        if t:
                            act.wait_ge(s[name + "s"], t)
                        act.activation(sqj[:], pair_bank(k, t), ACT.Square, accum_out=ss[:, t:t + 1]).then_inc(s[name + "s"], 1)
                        act.activation(halves(dst[:, t, :]), pair_bank(k, t), ACT.Copy).then_inc(s[name + "f"], 1)
                    act.wait_ge(s[name + "s"], NT)
                    act.activation(rn[:], ss[:], ACT.Sqrt).then_inc(s[name + "r"], 1)

                @block.vector
                def _(dve):
                    dve.wait_ge(s[name + "r"], 1)
                    dve.tensor_scalar(rn[:], rn[:], 1e-12, None, ALU.max).then_inc(s[name + "r"], 1)
                    dve.wait_ge(s[name + "r"], 2)
                    dve.reciprocal(rn[:], rn[:]).then_inc(s[name + "r"], 1)

        norms("k", k.XN, True)
        with nc.Block() as block:
            @block.sync
            def _(sp):
                sp.dma_start(W[:], third(2)).then_inc(s["wv"], 16)
                sp.wait_ge(s["wv"], 16)

            @block.tensor
            def _(pe):
                pe.wait_ge(s["wv"], 16)
                for t in range(NT + 1):
                    if t < NT:
                        if t >= 2:
                            pe.wait_ge(s["vf"], t - 1)
                        for h in range(2):
                            for c in range(KD):
                                mm = pe.matmul(k.PS[0:PT, 2 * (t % 2) + h, 0:HALF], k.FT[:, c, t * PT:(t + 1) * PT],
                                               W[:, c, h * HALF:(h + 1) * HALF], start=(c == 0), stop=(c == KD - 1))
                        mm.then_inc(s["v"], 1)
                    if t >= 1:
                        pe.wait_ge(s["vf"], t)
                        for h in range(2):
                            mm = pe.matmul(k.PS[0:PT, 4 + h, 0:HALF], k.ones[0:PT, 0:PT],
                                           kv[:, (t - 1) % 2, h * HALF:(h + 1) * HALF], start=(t == 1), stop=(t == NT))
                        mm.then_inc(s["kvt"], 1)

            @block.vector
            def _(dve):
                for t in range(NT):
                    dve.wait_ge(s["v"], t + 1)
                    if t >= 2:
                        dve.wait_ge(s["kvt"], t - 1)
                    dve.scalar_tensor_tensor(out=halves(kv[:, t % 2, :]), in0=pair_bank(k, t), scalar=rn[:, t:t + 1],
                                             in1=halves(k.XN[:, t, :]), op0=ALU.mult, op1=ALU.mult).then_inc(s["vf"], 1)
                dve.wait_ge(s["kvt"], NT)
                dve.tensor_copy(halves(kvB[:]), k.PS[0:PT, 4:6, 0:HALF]).then_inc(s["kvB"], 1)
        norms("q", k.XN, True)
        with nc.Block() as block:
            @block.vector
            def _(dve):
                for t in range(NT):
                    dve.scalar_tensor_tensor(out=k.XN[:, t, :], in0=k.XN[:, t, :], scalar=rn[:, t:t + 1], in1=kvB[:],
                                             op0=ALU.mult, op1=ALU.mult).then_inc(s["n"], 1)
    layernorm(nc, k, "lno", k.XN, k.XN, a["L1_mix_ln_out_g"], a["L1_mix_ln_out_b"])
    with ExitStack() as ctx:
        W = ctx.enter_context(nc.sbuf_tensor("lin_Wp", [128, KD, D], F32))
        with nc.Block() as block:
            @block.sync
            def _(sp):
                sp.dma_start(W[:], chunks_of(a["L1_mix_w_proj"])).then_inc(s["wp"], 16)
                sp.wait_ge(s["wp"], 16)

            @block.tensor
            def _(pe):
                pe.wait_ge(s["wp"], 16)
                rows_product(pe, k, k.FT, W, KD, D, s["y"], s["added"])

            @block.vector
            def _(dve):
                for t in range(NT):
                    dve.wait_ge(s["y"], t + 1)
                    dve.tensor_tensor(halves(k.X[:, t, :]), pair_bank(k, t), halves(k.X[:, t, :]), ALU.add)\
                        .then_inc(s["added"], 1)


def store(nc, k, out):
    stored = k.sem("x_stored")
    with nc.Block() as block:
        @block.sync
        def _(sp):
            sp.dma_start(rows_of(out), k.X[:]).then_inc(stored, 16)
            sp.wait_ge(stored, 16)


def program(nc, a, out):
    with ExitStack() as ctx:
        sb = lambda n, s, d=F32: ctx.enter_context(nc.sbuf_tensor(n, s, d))
        k = Kit()
        k.nc, k.sems = nc, []
        k.PS = ctx.enter_context(nc.psum_tensor("PS", [128, 8, 512], F32))
        k.X = sb("X", [PT, NT, D])
        k.XN = sb("XN", [PT, NT, D])
        k.FT = sb("FT", [128, KD, N])
        k.ident, k.ones = sb("ident", [128, 128]), sb("ones", [128, 128])
        k.sel, k.iota8 = sb("sel", [8, 8, PT]), sb("iota8", [PT, 8])
        k.comb, k.scrap = sb("comb", [PT, NT, 8]), sb("scrap", [1, 8])
        k.ln_eps = sb("ln_eps", [128, 1])
        epsd = k.sem("eps_made")
        with nc.Block() as block:
            @block.vector
            def _(dve):
                dve.memset(k.ln_eps[:], LN_EPS).then_inc(epsd, 1)
        setup(nc, k, a)

        layernorm(nc, k, "ln0", k.X, k.XN)
        with ExitStack() as c2:
            k.CT = c2.enter_context(nc.sbuf_tensor("CT", [PT, NT, N], F32))
            count_edges(nc, k, a)
            gcn(nc, k, a)
            with ExitStack() as c3:
                saved = k.sem("counts_saved")
                with nc.Block() as block:
                    @block.sync
                    def _(sp):
                        sp.dma_start(k.counts, k.CT[:]).then_inc(saved, 16)
                        sp.wait_ge(saved, 16)
        with ExitStack() as c2:
            k.HV = c2.enter_context(nc.sbuf_tensor("HV", [PT, NT, HEADS0, DH0 + 1], F32))
            with ExitStack() as c3:
                H = c3.enter_context(nc.sbuf_tensor("H", [PT, NT, D], F32))
                layernorm(nc, k, "ln1", k.XN, H, a["L0_mix_ln1_g"], a["L0_mix_ln1_b"], spare=k.HV)
            k.recycle()
            k.pdup = c2.enter_context(nc.sbuf_tensor("pdup", [128, 2, 2, DH0], F32))
            favor(nc, k, a)
        with ExitStack() as c2:
            H = c2.enter_context(nc.sbuf_tensor("H2", [PT, NT, D], F32))
            layernorm(nc, k, "ln2", k.XN, H, a["L0_mix_ln2_g"], a["L0_mix_ln2_b"])
            mlp(nc, k, "ffn0", a["L0_mix_W1"], a["L0_mix_b1"], ACT.Gelu, a["L0_mix_W2"], a["L0_mix_b2"],
                k.FT, KD, F0, extra=k.XN)
        k.recycle()
        layernorm(nc, k, "ln3", k.X, k.XN)
        router(nc, k, "rt0", a["L0_ffn_router_w"], None, EXP0, 2, a["L0_ffn_b_proj"], True)
        experts_mlp(nc, k, "moe0", a["L0_ffn_w_fc"], a["L0_ffn_b_fc"], a["L0_ffn_w_proj"], EXP0)

        k.recycle()
        layernorm(nc, k, "ln4", k.X, k.XN)
        with ExitStack() as c2:
            hx = c2.enter_context(nc.sbuf_tensor("hx1", [PT, NT, HEADS1, HID // HEADS1 + 1], F32))
            features(nc, k, "ft1", k.FT, KD, a["L1_gnn_W1"], hx, HEADS1, HID // HEADS1)
            with ExitStack() as c3:
                layernorm(nc, k, "ln5", k.XN, k.XN, a["L1_mix_ln_in_g"], a["L1_mix_ln_in_b"])
                linear_mixer(nc, k, a)
            k.recycle()
            G1 = k.XN[:].rearrange("p t d -> p (t d)")[:, 0:NT * HID].rearrange("p (t d) -> p t d", t=NT)
            GT = k.FT[:, 0:2, :]
            k.CT = c2.enter_context(nc.sbuf_tensor("CTb", [PT, NT, N], F32))
            back = k.sem("counts_back")
            with nc.Block() as block:
                @block.sync
                def _(sp):
                    sp.dma_start(k.CT[:], k.counts).then_inc(back, 16)
                    sp.wait_ge(back, 16)
            k.MK = c2.enter_context(nc.sbuf_tensor("MK", [PT, NT, N], BF16))
            mask(nc, k)
            with ExitStack() as c3:
                gat(nc, k, "gat1", a["L1_gnn_a_src1"], a["L1_gnn_a_dst1"], a["L1_gnn_b1"], hx, HEADS1,
                    HID // HEADS1, G1)
            turn(nc, k, "tn1", G1, GT, 2)
            hx2 = hx[:].rearrange("p t h d -> p t (h d)")[:, :, 0:HID + 1].rearrange("p t (o d) -> p t o d", o=1)
            features(nc, k, "ft2", GT, 2, a["L1_gnn_W2"], hx2, 1, HID)
            gat(nc, k, "gat2", a["L1_gnn_a_src2"], a["L1_gnn_a_dst2"], a["L1_gnn_b2"], hx2, 1, HID, G1)
            turn(nc, k, "tn2", G1, GT, 2)
            mlp(nc, k, "gmlp", a["L1_gnn_Wm1"], a["L1_gnn_bm1"], ACT.Relu, a["L1_gnn_Wm2"], a["L1_gnn_bm2"],
                GT, 2, HID)
        k.recycle()
        layernorm(nc, k, "ln6", k.X, k.XN)
        router(nc, k, "rt1", a["L1_ffn_Wg"], a["L1_ffn_bg"], EXP1, 1, a["L1_ffn_b2"], False)
        experts_mlp(nc, k, "moe1", a["L1_ffn_W1"], a["L1_ffn_b1"], a["L1_ffn_W2"], EXP1)
        store(nc, k, out)


def kernel(**inputs):
    import numpy as np
    import concourse.bacc as bacc
    from concourse.bass_utils import run_bass_kernel_spmd as run

    nc = bacc.Bacc("TRN2", target_bir_lowering=False, num_devices=1)
    arrays, a = {}, {}
    for name, value in inputs.items():
        v = np.ascontiguousarray(value)
        arrays["in_" + name] = v
        a[name] = nc.dram_tensor("in_" + name, v.shape, mybir.dt.from_np(v.dtype), kind="ExternalInput").ap()
    out = nc.dram_tensor("out", (N, D), F32, kind="ExternalOutput").ap()
    Kit.counts = nc.dram_tensor("counts", (PT, NT, N), F32, kind="Internal").ap()
    program(nc, a, out)
    r = run(nc, [arrays], core_ids=[0])
    return r.results[0]["out"]
```

```python
from contextlib import ExitStack

import concourse.bass as bass
from concourse import mybir

F32 = mybir.dt.float32
BF16 = mybir.dt.bfloat16
F16 = mybir.dt.float16
I32 = mybir.dt.int32
U32 = mybir.dt.uint32
ALU = mybir.AluOpType
ACT = mybir.ActivationFunctionType
AX = mybir.AxisListType

N, D = 1250, 768
PT = 125
NT = N // PT
KD = D // 128
HALF = D // 2
CHUNKS = ((0, 500), (500, 500), (1000, 250))
E = 20000
EC = E // PT
EPER = 4
EGROUP = EPER * PT
EGROUPS = 50
assert EGROUPS >= (E + NT * (EGROUP - 1)) // EGROUP and EGROUPS % 2 == 0
WORD_BITS = 11
WORD = 1 << WORD_BITS
HEADS0, DH0, M0 = 12, 64, 256
F0, EXP0 = 384, 8
KF = F0 // 128
HID, HEADS1 = 256, 4
EXP1 = 4
MOST = 2 * NT + EXP0 - 1
LN_EPS = 1e-5
EPS0 = 1e-4
SC0 = DH0 ** -0.25
NEG = -1e30


class Chain:

    def __init__(self, eng, sem, base=0):
        self.eng, self.sem, self.base, self.n = eng, sem, base, 0

    def __call__(self, ins):
        self.n += 1
        ins.then_inc(self.sem, 1)
        self.eng.wait_ge(self.sem, self.base + self.n)


class Kit:

    def sem(self, name):
        self.sems.append(self.nc.alloc_semaphore(name=name))
        return self.sems[-1]

    def gpsimd_dma_sem(self, name):
        return self.nc.alloc_semaphore(name=name)

    def recycle(self):
        nums = sorted(s.num for s in self.sems)
        runs = [[nums[0], nums[0]]]
        for n in nums[1:]:
            if n == runs[-1][1] + 1:
                runs[-1][1] = n
            else:
                runs.append([n, n])
        with self.nc.Block() as block:
            @block.gpsimd
            def _(pool):
                for lo, hi in runs:
                    pool.sem_clear(range(lo, hi + 1))
        for s in self.sems:
            self.nc.release_semaphore(s)
        self.sems = []


def rows_of(dram):
    return dram.rearrange("(t p) d -> p t d", p=PT)


def chunks_of(dram):
    return dram.rearrange("(k p) n -> p k n", p=128)


def spread(dram, n):
    return dram.rearrange("(a n) -> a n", a=1).to_broadcast([PT, n])


def setup(nc, k, a):
    zeroed, made, loaded = k.sem("zeroed"), k.sem("made"), k.sem("x_loaded")
    with nc.Block() as block:
        @block.sync
        def _(sp):
            sp.dma_start(k.X[:], rows_of(a["x"])).then_inc(loaded, 16)
            sp.wait_ge(loaded, 16)

        @block.gpsimd
        def _(pool):
            pool.memset(k.ident[:], 0.0).then_inc(zeroed, 1)
            pool.memset(k.ones[:], 1.0).then_inc(made, 1)
            pool.memset(k.sel[:], 0.0).then_inc(zeroed, 1)
            pool.wait_ge(zeroed, 2)
            pool.affine_select(out=k.ident[:], in_=k.ident[:], compare_op=ALU.not_equal, fill=1.0, base=0,
                               pattern=[[-1, 128]], channel_multiplier=1).then_inc(made, 1)
            pool.affine_select(out=k.sel[:], in_=k.sel[:], compare_op=ALU.not_equal, fill=1.0, base=0,
                               pattern=[[-1, 8], [0, PT]], channel_multiplier=1).then_inc(made, 1)
            pool.iota(k.iota[:], pattern=[[1, 64]], base=0, channel_multiplier=0,
                      allow_small_or_imprecise_dtypes=True).then_inc(made, 1)
            pool.iota(k.node[:], pattern=[[PT, NT]], base=0, channel_multiplier=1).then_inc(made, 1)
            pool.memset(k.before[:], 1.0).then_inc(zeroed, 1)
            pool.wait_ge(zeroed, 3)
            pool.affine_select(out=k.before[:], in_=k.before[:], compare_op=ALU.is_gt, fill=0.0, base=0,
                               pattern=[[1, PT]], channel_multiplier=-1).then_inc(made, 1)
            pool.wait_ge(made, 6)


def layernorm(nc, k, name, src, dst, gain=None, shift=None, spare=None):
    stats, aggregated, deviation, inverse = (k.sem(f"{name}_{s}") for s in ("stats", "aggr", "std", "rstd"))
    normal, turned, stored, steps, loaded = (k.sem(f"{name}_{s}") for s in ("normal", "turned", "stored", "steps", "affine"))
    spared = k.sem(f"{name}_spared")
    with ExitStack() as ctx:
        st = ctx.enter_context(nc.sbuf_tensor(f"{name}_st", [PT, NT, 2, 6], F32))
        mv = ctx.enter_context(nc.sbuf_tensor(f"{name}_mv", [PT, NT, 2], F32))
        std = ctx.enter_context(nc.sbuf_tensor(f"{name}_sd", [PT, NT], F32))
        rstd = ctx.enter_context(nc.sbuf_tensor(f"{name}_rs", [PT, NT], F32))
        gb = ctx.enter_context(nc.sbuf_tensor(f"{name}_gb", [PT, 2, D], F32)) if gain is not None else None
        with nc.Block() as block:
            if gain is not None:
                @block.sync
                def _(sp):
                    sp.dma_start(gb[:, 0, :], spread(gain, D)).then_inc(loaded, 16)
                    sp.dma_start(gb[:, 1, :], spread(shift, D)).then_inc(loaded, 16)
                    sp.wait_ge(loaded, 32)

            @block.vector
            def _(dve):
                with dve.Fori(0, NT) as t:
                    for h in range(2):
                        dve.bn_stats(st[:, t, h, :], src[:, t, h * HALF:(h + 1) * HALF]).then_inc(stats, 1)
                dve.wait_ge(stats, 2 * NT)
                for t in range(NT):
                    dve.bn_aggr(mv[:, t, :], st[:, t, :, :]).then_inc(aggregated, 1)
                dve.wait_ge(deviation, 1)
                dve.reciprocal(rstd[:], std[:]).then_inc(inverse, 1)
                dve.wait_ge(inverse, 1)
                if gain is not None:
                    dve.wait_ge(loaded, 32)
                for t in range(NT):
                    link = Chain(dve, steps, 2 * t)
                    last = dve.tensor_scalar(dst[:, t, :], src[:, t, :], mv[:, t, 0:1], rstd[:, t:t + 1],
                                             ALU.subtract, ALU.mult)
                    if gain is not None:
                        link(last)
                        link(dve.tensor_tensor(dst[:, t, :], dst[:, t, :], gb[:, 0, :], ALU.mult))
                        last = dve.tensor_tensor(dst[:, t, :], dst[:, t, :], gb[:, 1, :], ALU.add)
                    last.then_inc(normal, 1)

            @block.scalar
            def _(act):
                act.wait_ge(aggregated, NT)
                act.activation(std[:].rearrange("p (t o) -> p t o", o=1), mv[:, :, 1:2], ACT.Sqrt,
                               bias=k.ln_eps[0:PT, :]).then_inc(deviation, 1)
                for t in range(NT):
                    act.wait_ge(turned, t + 1)
                    act.activation(k.FT[:, :, t * PT:(t + 1) * PT].rearrange("p (a b) n -> p a b n", a=2),
                                   k.PS[:, 2 * (t % 2):2 * (t % 2) + 2, 0:3 * PT].rearrange("p a (b n) -> p a b n", b=3),
                                   ACT.Copy).then_inc(stored, 1)

            if spare is not None:
                @block.gpsimd
                def _(pool):
                    pool.memset(spare[:, :, :, DH0:DH0 + 1], 1.0).then_inc(spared, 1)
                    for t in range(NT):
                        pool.wait_ge(normal, t + 1)
                        pool.tensor_copy(spare[:, t, :, 0:DH0],
                                         dst[:, t, :].rearrange("p (h d) -> p h d", d=DH0)).then_inc(spared, 1)

            @block.tensor
            def _(pe):
                for t in range(NT):
                    pe.wait_ge(normal, t + 1)
                    if t >= 2:
                        pe.wait_ge(stored, t - 1)
                    for c in range(KD):
                        mm = pe.transpose(k.PS[:, 2 * (t % 2) + c // 3, (c % 3) * PT:(c % 3 + 1) * PT],
                                          dst[:, t, c * 128:(c + 1) * 128], k.ident[0:PT, 0:PT])
                    mm.then_inc(turned, 1)


def turn(nc, k, name, src, dst, chunks):
    turned, stored = k.sem(f"{name}_turned"), k.sem(f"{name}_stored")
    with nc.Block() as block:
        @block.tensor
        def _(pe):
            for t in range(NT):
                if t >= 2:
                    pe.wait_ge(stored, t - 1)
                for c in range(chunks):
                    mm = pe.transpose(k.PS[:, t % 2, c * PT:(c + 1) * PT], src[:, t, c * 128:(c + 1) * 128],
                                      k.ident[0:PT, 0:PT])
                mm.then_inc(turned, 1)

        @block.scalar
        def _(act):
            for t in range(NT):
                act.wait_ge(turned, t + 1)
                act.activation(dst[:, :, t * PT:(t + 1) * PT],
                               k.PS[:, t % 2, 0:chunks * PT].rearrange("p (c n) -> p c n", c=chunks),
                               ACT.Copy).then_inc(stored, 1)


def rows_product(pe, k, lhs, rhs, chunks, width, ready, freed, base=0):
    for t in range(NT):
        if t >= 2:
            pe.wait_ge(freed, base + t - 1)
        for h in range(2):
            for c in range(chunks):
                mm = pe.matmul(k.PS[0:PT, 2 * (t % 2) + h, 0:width // 2], lhs[:, c, t * PT:(t + 1) * PT],
                               rhs[:, c, h * (width // 2):(h + 1) * (width // 2)],
                               start=(c == 0), stop=(c == chunks - 1))
        mm.then_inc(ready, 1)


def pair_bank(k, t, width=D):
    return k.PS[0:PT, 2 * (t % 2):2 * (t % 2) + 2, 0:width // 2]


def halves(ap):
    return ap.rearrange("p (a n) -> p a n", a=2)


def place_edges(nc, k, a):
    loaded, steps = k.sem("edges_loaded"), k.sem("edges_steps")
    with ExitStack() as ctx:
        sb = lambda n, sh, d=F32: ctx.enter_context(nc.sbuf_tensor(n, sh, d))
        raw, ends = sb("edges_raw", [PT, 2, EC], I32), sb("edges_f", [PT, 2, EC])
        firsts, past, tile = sb("tile_firsts", [PT, NT - 1]), sb("edges_past", [PT, EC, NT - 1]), sb("edges_tile", [PT, EC])
        with nc.Block() as block:
            @block.sync
            def _(sp):
                sp.dma_start(raw[:, 0, :], a["src"].rearrange("(p c) -> p c", c=EC)).then_inc(loaded, 16)
                sp.dma_start(raw[:, 1, :], a["dst"].rearrange("(p c) -> p c", c=EC)).then_inc(loaded, 16)
                sp.wait_ge(loaded, 32)

            @block.vector
            def _(dve):
                link = Chain(dve, steps)
                dve.wait_ge(loaded, 32)
                link(dve.tensor_copy(ends[:], raw[:]))
                link(dve.tensor_scalar(firsts[:], k.iota[:, 1:NT], float(PT), None, ALU.mult))
                link(dve.tensor_tensor(past[:], ends[:, 0, :].rearrange("p (c o) -> p c o", o=1)
                                       .to_broadcast([PT, EC, NT - 1]),
                                       firsts[:].rearrange("p (o j) -> p o j", o=1).to_broadcast([PT, EC, NT - 1]),
                                       ALU.is_ge))
                link(dve.tensor_reduce(tile[:], past[:], AX.X, ALU.add))
                link(dve.scalar_tensor_tensor(out=ends[:, 0, :], in0=tile[:], scalar=-float(PT), in1=ends[:, 0, :],
                                              op0=ALU.mult, op1=ALU.add))
                link(dve.scalar_tensor_tensor(out=ends[:, 1, :], in0=ends[:, 0, :], scalar=float(WORD),
                                              in1=ends[:, 1, :], op0=ALU.mult, op1=ALU.add))
                link(dve.tensor_copy(k.KEY[:], ends[:, 1, :]))
        bin_items(nc, k, "edge_bin", tile[:], EC, NT, EGROUP, EGROUPS, k.EPOS[:], k.ETILE[:])


def scatter_edges(nc, k):
    k.edges_placed = k.gpsimd_dma_sem("edges_placed")

    def scatter(pool):
        for c in range(EC):
            pool.indirect_dma_start(out=k.edge_list, out_offset=bass.IndirectOffsetOnAxis(ap=k.EPOS[:, c:c + 1], axis=0),
                                    in_=k.KEY[:, c:c + 1], in_offset=None).then_inc(k.edges_placed, 16)
        pool.wait_ge(k.edges_placed, 16 * EC)
    return scatter


def clear_edge_list(nc, k):
    filled, cleared = k.sem("edge_fill"), k.sem("edges_cleared")
    with ExitStack() as ctx:
        fill = ctx.enter_context(nc.sbuf_tensor("edge_fill_words", [PT, EPER * EGROUPS], U32))
        with nc.Block() as block:
            @block.vector
            def _(dve):
                dve.memset(fill[:], (PT + 1) * WORD).then_inc(filled, 1)

            @block.sync
            def _(sp):
                sp.wait_ge(filled, 1)
                sp.dma_start(k.edge_list.rearrange("(p n) o -> p (n o)", p=PT), fill[:]).then_inc(cleared, 16)
                sp.wait_ge(cleared, 16)


def count_edges(nc, k, HS):
    loaded, split, iotas, hot, freed, moved, added, zeroed = (
        k.sem(f"count_{s}") for s in ("loaded", "split", "iota", "hot", "freed", "moved", "added", "zeroed"))
    restored = k.sem("features_restored")
    SLOTS = 8
    with ExitStack() as ctx:
        sb = lambda n, sh, d=F32: ctx.enter_context(nc.sbuf_tensor(n, sh, d))
        words, parts = sb("edge_words", [PT, EGROUPS, EPER], U32), sb("edge_parts", [PT, 2, EGROUPS, EPER], U32)
        ends = sb("edge_ends", [PT, 2, EGROUPS * EPER])
        iota = sb("iota_nodes", [PT, N], F16)
        hd, hs = sb("dst_hot", [PT, SLOTS, N], BF16), sb("src_hot", [PT, SLOTS, PT], BF16)
        part = sb("count_part", [PT, 2, N])
        with nc.Block() as block:
            @block.sync
            def _(sp):
                sp.dma_start(words[:], k.edge_list.rearrange("(g p c) o -> p g (c o)", p=PT, c=EPER)).then_inc(loaded, 16)
                sp.dma_start(HS[:], rows_of(k.features)).then_inc(restored, 16)
                sp.wait_ge(restored, 16)

            @block.gpsimd
            def _(pool):
                pool.iota(iota[:], pattern=[[1, N]], base=0, channel_multiplier=0,
                          allow_small_or_imprecise_dtypes=True).then_inc(iotas, 1)
                pool.memset(k.CT[:], 0.0).then_inc(zeroed, 1)
                pool.wait_ge(zeroed, 1)
                for g in range(EGROUPS):
                    tile = pool.value_load(k.ETILE[0:1, g:g + 1], min_val=0, max_val=NT - 1)
                    rows = k.CT[:, bass.ds(tile, 1), :].rearrange("p o n -> p (o n)")
                    pool.wait_ge(moved, 2 + g + 1)
                    if g:
                        pool.wait_ge(added, g)
                    pool.tensor_tensor(rows, rows, part[:, g % 2, :], ALU.add).then_inc(added, 1)

            @block.vector
            def _(dve):
                dve.wait_ge(loaded, 16)
                flat = words[:].rearrange("p g c -> p (g c)")
                halves_of = parts[:].rearrange("p a g c -> p a (g c)")
                dve.tensor_scalar(halves_of[:, 0, :], flat, WORD_BITS, None, ALU.logical_shift_right).then_inc(split, 1)
                dve.tensor_scalar(halves_of[:, 1, :], flat, WORD - 1, None, ALU.bitwise_and).then_inc(split, 1)
                dve.wait_ge(split, 2)
                dve.tensor_copy(ends[:], halves_of).then_inc(split, 1)
                dve.wait_ge(split, 3)
                dve.wait_ge(iotas, 1)
                with dve.Fori(0, EGROUPS * EPER // SLOTS) as turn_:
                    for s in range(SLOTS):
                        c = SLOTS * turn_ + s
                        dve.wait_ge(freed, c + 1)
                        dve.tensor_scalar(hs[:, s, :], iota[:, 0:PT], ends[:, 0, bass.ds(c, 1)], None,
                                          ALU.is_equal).then_inc(hot, 1)
                        dve.tensor_scalar(hd[:, s, :], iota[:], ends[:, 1, bass.ds(c, 1)], None,
                                          ALU.is_equal).then_inc(hot, 1)

            @block.tensor
            def _(pe):
                pe.matmul(k.PS[0:1, 7, 0:64], k.ident[:, 0:1], k.ident[:, 0:64], start=True, stop=True)\
                    .then_inc(freed, SLOTS)
                with pe.Fori(0, EGROUPS * EPER // SLOTS) as turn_:
                    for i in range(SLOTS // EPER):
                        g = (SLOTS // EPER) * turn_ + i
                        pe.wait_ge(moved, g + 1)
                        for c in range(EPER):
                            s = EPER * i + c
                            pe.wait_ge(hot, 2 * (SLOTS * turn_ + (s + 1)))
                            for b, (lo, n) in enumerate(CHUNKS):
                                mm = pe.matmul(k.PS[0:PT, 3 * i + b, 0:n], hs[:, s, :], hd[:, s, lo:lo + n],
                                               start=(c == 0), stop=(c == EPER - 1))
                            mm.then_inc(freed, 1)

            @block.scalar
            def _(act):
                act.activation(k.scrap[0:1, 2:3], k.ones[0:1, 0:1], ACT.Copy).then_inc(moved, 2)
                for g in range(EGROUPS):
                    act.wait_ge(freed, SLOTS + EPER * (g + 1))
                    if g >= 2:
                        act.wait_ge(added, g - 1)
                    for b, (lo, n) in enumerate(CHUNKS):
                        ins = act.activation(part[:, g % 2, lo:lo + n], k.PS[0:PT, 3 * (g % 2) + b, 0:n], ACT.Copy)
                        if b == 2:
                            ins.then_inc(moved, 1)
        with nc.Block() as block:
            @block.vector
            def _(dve):
                for t in range(NT):
                    blk = k.CT[:, t, t * PT:(t + 1) * PT]
                    dve.tensor_tensor(blk, blk, k.ident[0:PT, 0:PT], ALU.add).then_inc(split, 1)


def gcn_features(nc, k, a):
    loaded, made, stored, kept = (k.sem(f"gcn_{s}") for s in ("w", "made", "stored", "kept"))
    with ExitStack() as ctx:
        HS = ctx.enter_context(nc.sbuf_tensor("HS_made", [PT, NT, D], F32))
        W = ctx.enter_context(nc.sbuf_tensor("gcn_W", [128, KD, D], F32))
        with nc.Block() as block:
            @block.sync
            def _(sp):
                sp.dma_start(W[:], chunks_of(a["L0_gnn_W"])).then_inc(loaded, 16)
                sp.wait_ge(stored, NT)
                sp.dma_start(rows_of(k.features), HS[:]).then_inc(kept, 16)
                sp.wait_ge(kept, 16)

            @block.tensor
            def _(pe):
                pe.wait_ge(loaded, 16)
                rows_product(pe, k, k.FT, W, KD, D, made, stored)

            @block.scalar
            def _(act):
                for t in range(NT):
                    act.wait_ge(made, t + 1)
                    act.activation(halves(HS[:, t, :]), pair_bank(k, t), ACT.Copy).then_inc(stored, 1)


def gcn(nc, k, a, HS):
    loaded, degreed, rooted, inverted, scaled, summed, added, biased = (
        k.sem(f"gcn_{s}") for s in ("loaded", "deg", "root", "dinv", "scaled", "summed", "added", "biased"))
    with ExitStack() as ctx:
        bias = ctx.enter_context(nc.sbuf_tensor("gcn_b", [PT, D], F32))
        root = ctx.enter_context(nc.sbuf_tensor("gcn_root", [PT, NT], F32))
        dinv = ctx.enter_context(nc.sbuf_tensor("gcn_dinv", [PT, NT], F32))
        with nc.Block() as block:
            @block.sync
            def _(sp):
                sp.dma_start(bias[:], spread(a["L0_gnn_b"], D)).then_inc(loaded, 16)
                sp.wait_ge(loaded, 16)

            @block.tensor
            def _(pe):
                for d in range(NT):
                    for s in range(NT):
                        mm = pe.matmul(k.PS[0:PT, 7, d:d + 1], k.CT[:, s, d * PT:(d + 1) * PT], k.ones[0:PT, 0:1],
                                       start=(s == 0), stop=(s == NT - 1))
                mm.then_inc(degreed, 1)
                pe.wait_ge(scaled, NT)
                for d in range(NT):
                    if d >= 2:
                        pe.wait_ge(added, d - 1)
                    for h in range(2):
                        for s in range(NT):
                            mm = pe.matmul(k.PS[0:PT, 2 * (d % 2) + h, 0:HALF], k.CT[:, s, d * PT:(d + 1) * PT],
                                           HS[:, s, h * HALF:(h + 1) * HALF], start=(s == 0), stop=(s == NT - 1))
                    mm.then_inc(summed, 1)

            @block.scalar
            def _(act):
                act.wait_ge(degreed, 1)
                act.activation(root[:], k.PS[0:PT, 7, 0:NT], ACT.Sqrt).then_inc(rooted, 1)
                act.wait_ge(inverted, 1)
                for t in range(1, NT, 2):
                    act.activation(HS[:, t, :], HS[:, t, :], ACT.Copy, scale=dinv[:, t:t + 1]).then_inc(scaled, 1)

            @block.vector
            def _(dve):
                dve.wait_ge(rooted, 1)
                dve.reciprocal(dinv[:], root[:]).then_inc(inverted, 1)
                dve.wait_ge(inverted, 1)
                for t in range(0, NT, 2):
                    dve.tensor_scalar(HS[:, t, :], HS[:, t, :], dinv[:, t:t + 1], None, ALU.mult).then_inc(scaled, 1)
                for t in range(NT):
                    dve.wait_ge(biased, t + 1)
                    dve.wait_ge(summed, t + 1)
                    dve.scalar_tensor_tensor(out=halves(k.X[:, t, :]), in0=pair_bank(k, t), scalar=dinv[:, t:t + 1],
                                             in1=halves(k.X[:, t, :]), op0=ALU.mult, op1=ALU.add).then_inc(added, 1)

            @block.gpsimd
            def _(pool):
                pool.wait_ge(loaded, 16)
                for t in range(NT):
                    pool.tensor_tensor(k.X[:, t, :], k.X[:, t, :], bias[:], ALU.add).then_inc(biased, 1)


def favor(nc, k, a, background=None):
    names = ("loaded", "copied", "u", "max", "bias", "peak", "peakT", "top", "spread", "shift", "decay", "q", "kp",
             "turned", "qt", "ctx", "cx", "num", "rden", "tmp", "added", "proj", "projT", "sq", "eps")
    s = {n: k.sem(f"fav_{n}") for n in names}
    SC = SC0
    with ExitStack() as ctx:
        sb = lambda n, sh: ctx.enter_context(nc.sbuf_tensor(n, sh, F32))
        HV, htp, eps, proj = k.HV, sb("fav_htp", [128, 2, N]), sb("fav_eps", [128, 1]), sb("fav_proj", [128, M0])
        QE, KP, QT = sb("fav_QE", [PT, 2, NT, M0]), sb("fav_KP", [PT, NT, M0]), sb("fav_QT", [128, 2, N])
        CX, DG, sq = sb("fav_CX", [128, 2, DH0 + 1]), sb("fav_DG", [PT, NT, HEADS0]), sb("fav_sq", [PT, HEADS0, DH0])
        RM, NB, SK, pk, g1, NK = (sb("fav_RM", [PT, 2, NT]), sb("fav_NB", [PT, 2, NT]), sb("fav_SK", [PT, NT]),
                                  sb("fav_pk", [PT, 1]), sb("fav_g1", [1, 1]), sb("fav_NK", [PT, 1]))
        RD, TM = sb("fav_RD", [PT, NT]), sb("fav_TM", [PT, NT, DH0])
        U = k.PS[0:PT, 0:2, :].rearrange("p b (c m) -> p b c m", c=2)
        NUM = k.PS[0:PT, 4:6, 0:5 * (DH0 + 1)].rearrange("p b (c m) -> p b c m", c=5)
        CTX = k.PS[:, 7, 256:256 + 2 * (DH0 + 1)].rearrange("p (m d) -> p m d", m=2)
        with nc.Block() as block:
            @block.sync
            def _(sp):
                pv = a["L0_mix_proj"].rearrange("(c p) d -> p c d", p=128)
                for j in range(2):
                    sp.dma_start(k.pdup[:, :, j, :], pv).then_inc(s["loaded"], 16)
                sp.wait_ge(s["loaded"], 32)

            @block.tensor
            def _(pe):
                pe.wait_ge(s["loaded"], 32)
                for c in range(2):
                    mm = pe.transpose(k.PS[:, 7, c * 128:(c + 1) * 128],
                                      k.pdup[:, c, :, :].rearrange("p a d -> p (a d)"), k.ident[:])
                mm.then_inc(s["proj"], 1)

            @block.vector
            def _(dve):
                dve.wait_ge(s["proj"], 1)
                dve.tensor_copy(proj[:], k.PS[:, 7, 0:256]).then_inc(s["projT"], 1)
                for t in range(NT):
                    link = Chain(dve, s["sq"], 2 * t)
                    link(dve.tensor_tensor(sq[:], HV[:, t, :, 0:DH0], HV[:, t, :, 0:DH0], ALU.mult))
                    link(dve.tensor_reduce(DG[:, t, :], sq[:], AX.X, ALU.add))
                dve.tensor_scalar(DG[:], DG[:], 0.5 * SC * SC, None, ALU.mult).then_inc(s["sq"], 1)
        with nc.Block() as block:
            QUADS = HEADS0 // 4
            G5 = NT // 2

            if background is not None:
                @block.gpsimd
                def _(pool):
                    background(pool)

            @block.tensor
            def _(pe):
                def turn_q(h, j, g):
                    pe.wait_ge(s["q"], G5 * h + (g + 3))
                    pe.wait_ge(s["qt"], G5 * h + (g + 1))
                    for m in range(2):
                        for i in range(2):
                            mm = pe.transpose(k.PS[:, 2 + (5 * j + g) % 2, (2 * m + i) * PT:(2 * m + i + 1) * PT],
                                              QE[:, j % 2, 2 * g + i, m * 128:(m + 1) * 128], k.ident[0:PT, 0:PT])
                    mm.then_inc(s["turned"], 1)

                def quad(h0, last):
                    for j in range(4):
                        h = h0 + j
                        pe.wait_ge(s["peak"], h + 1)
                        pe.transpose(k.PS[0:1, 7, 0:PT], pk[:], k.ident[0:PT, 0:PT]).then_inc(s["peakT"], 1)
                        for g in range(G5):
                            if not (last and j == 3):
                                score(h + 1, (j + 1) % 4, g) if j < 3 else score_next(h + 1, g)
                            turn_q(h, j, g)
                            if g == 0:
                                pe.wait_ge(s["top"], h + 1)
                                pe.matmul(k.PS[0:PT, 7, 128:129], k.ones[0:1, 0:PT], g1[:], start=True, stop=True)\
                                    .then_inc(s["spread"], 1)
                        pe.wait_ge(s["kp"], G5 * h + G5)
                        for m in range(2):
                            for t in range(NT):
                                mm = pe.matmul(CTX[:, m, :], KP[:, t, m * 128:(m + 1) * 128],
                                               HV[:, t, bass.ds(h, 1), :].rearrange("p o d -> p (o d)"),
                                               start=(t == 0), stop=(t == NT - 1))
                        mm.then_inc(s["ctx"], 1)
                        pe.wait_ge(s["cx"], h + 1)
                        pe.wait_ge(s["qt"], G5 * h + (G5 + 2))
                        pe.wait_ge(s["tmp"], h + 1)
                        for t in range(NT):
                            for m in range(2):
                                mm = pe.matmul(NUM[:, t // 5, t % 5, :], QT[:, m, t * PT:(t + 1) * PT], CX[:, m, :],
                                               start=(m == 0), stop=(m == 1))
                        mm.then_inc(s["num"], 1)

                def score_next(h, g):
                    pe.wait_ge(s["q"], G5 * h + (g + 1))
                    if g == 0:
                        pe.wait_ge(s["copied"], next_pair[0])
                    for i in range(2):
                        t = 2 * g + i
                        mm = pe.matmul(U[:, g % 2, i, :], htp[0:DH0, 0, t * PT:(t + 1) * PT], proj[0:DH0, :],
                                       start=True, stop=True)
                    mm.then_inc(s["u"], 1)

                next_pair = [None]

                def score(h, j, g):
                    pe.wait_ge(s["q"], G5 * h + (g + 1))
                    if g == 0:
                        pe.wait_ge(s["copied"], this_pair[0] + (j // 2 + 1))
                    lo = DH0 * (j % 2)
                    for i in range(2):
                        t = 2 * g + i
                        mm = pe.matmul(U[:, (5 * j + g) % 2, i, :], htp[lo:lo + DH0, j // 2, t * PT:(t + 1) * PT],
                                       proj[lo:lo + DH0, :], start=True, stop=True)
                    mm.then_inc(s["u"], 1)

                this_pair = [0]
                for g in range(G5):
                    score(0, 0, g)
                with pe.Fori(0, QUADS - 1) as q:
                    this_pair[0], next_pair[0] = 2 * q, 2 * q + 3
                    quad(4 * q, False)
                this_pair[0] = 2 * (QUADS - 1)
                quad(4 * (QUADS - 1), True)

            @block.scalar
            def _(act):
                act.preload_act_table(ACT.Exp)
                act.activation(k.scrap[0:1, 2:3], k.ones[0:1, 0:1], ACT.Copy).then_inc(s["q"], 2)
                act.activation(k.scrap[0:1, 3:4], k.ones[0:1, 0:1], ACT.Copy).then_inc(s["qt"], 2)

                def exps(h, j, g):
                    act.wait_ge(s["bias"], G5 * h + (g + 1))
                    for i in range(2):
                        t = 2 * g + i
                        ins = act.activation(QE[:, j % 2, t, :], U[:, (5 * j + g) % 2, i, :], ACT.Exp, scale=SC,
                                             bias=NB[:, j % 2, t:t + 1])
                    ins.then_inc(s["q"], 1)

                def quad(h0, pair0, last):
                    for j in range(4):
                        h = h0 + j
                        if j % 2 == 0 and not (last and j == 2):
                            act.activation(htp[:, (j // 2 + 1) % 2, :], k.FT[:, bass.ds(pair0 + (j // 2 + 1), 1), :]
                                           .rearrange("p o n -> p (o n)"), ACT.Copy).then_inc(s["copied"], 1)
                        for g in range(G5):
                            if not (last and j == 3):
                                exps(h + 1, (j + 1) % 4, g)
                            act.wait_ge(s["turned"], G5 * h + (g + 1))
                            act.activation(QT[:, :, 2 * g * PT:(2 * g + 2) * PT],
                                           k.PS[:, 2 + (5 * j + g) % 2, 0:4 * PT].rearrange("p (m n) -> p m n", m=2),
                                           ACT.Identity, bias=eps[:]).then_inc(s["qt"], 1)
                            if g == 1:
                                act.wait_ge(s["shift"], h + 1)
                                act.activation(SK[:], RM[:, j % 2, :], ACT.Exp, scale=SC, bias=NK[:]).then_inc(s["decay"], 1)
                        act.wait_ge(s["ctx"], h + 1)
                        act.activation(CX[:], CTX, ACT.Copy).then_inc(s["cx"], 1)

                act.activation(htp[:, 0, :], k.FT[:, 0, :], ACT.Copy).then_inc(s["copied"], 1)
                for g in range(G5):
                    exps(0, 0, g)
                with act.Fori(0, QUADS - 1) as q:
                    quad(4 * q, 2 * q, False)
                quad(4 * (QUADS - 1), 2 * (QUADS - 1), True)

            @block.vector
            def _(dve):
                dve.memset(eps[:], EPS0).then_inc(s["eps"], 1)
                dve.memset(k.scrap[0:1, 0:1], 0.0).then_inc(s["tmp"], 1)

                def biases(h, j, g):
                    dve.wait_ge(s["u"], G5 * h + (g + 1))
                    rm = RM[:, j % 2, 2 * g:2 * g + 2]
                    dve.tensor_reduce(rm, U[:, (5 * j + g) % 2, :, :], AX.X, ALU.max).then_inc(s["max"], 1)
                    dve.wait_ge(s["max"], G5 * h + (g + 1))
                    dve.scalar_tensor_tensor(out=NB[:, j % 2, 2 * g:2 * g + 2].rearrange("p (t o) -> p t o", o=1),
                                             in0=rm.rearrange("p (t o) -> p t o", o=1), scalar=-SC,
                                             in1=DG[:, 2 * g:2 * g + 2, bass.ds(h, 1)], op0=ALU.mult,
                                             op1=ALU.subtract).then_inc(s["bias"], 1)
                    if g == G5 - 1:
                        dve.reduce_max(pk[:], RM[:, j % 2, :], AX.X).then_inc(s["peak"], 1)

                def finish(h):
                    dve.wait_ge(s["num"], h + 1)
                    dve.reciprocal(RD[:].rearrange("p (b c o) -> p b c o", b=2, o=1), NUM[:, :, :, DH0:DH0 + 1])\
                        .then_inc(s["rden"], 1)
                    dve.wait_ge(s["rden"], h + 1)
                    dve.tensor_tensor(TM[:].rearrange("p (b c) d -> p b c d", b=2), NUM[:, :, :, 0:DH0],
                                      RD[:].rearrange("p (b c o) -> p b c o", b=2, o=1).to_broadcast([PT, 2, 5, DH0]),
                                      ALU.mult).then_inc(s["tmp"], 1)
                    dve.wait_ge(s["tmp"], h + 2)
                    xs = k.XN[:, :, bass.ds(h * DH0, DH0)]
                    dve.tensor_tensor(xs, xs, TM[:], ALU.add).then_inc(s["added"], 1)

                def quad(h0, first, last):
                    for j in range(4):
                        h = h0 + j
                        dve.wait_ge(s["peakT"], h + 1)
                        dve.reduce_max(g1[:], k.PS[0:1, 7, 0:PT], AX.X).then_inc(s["top"], 1)
                        for g in range(G5):
                            if not (last and j == 3):
                                biases(h + 1, (j + 1) % 4, g)
                            if g == 0:
                                dve.wait_ge(s["spread"], h + 1)
                                dve.tensor_scalar(NK[:], k.PS[0:PT, 7, 128:129], -SC, None, ALU.mult)\
                                    .then_inc(s["shift"], 1)
                            if g == 2 and not (first and j == 0):
                                finish(h - 1)
                            if g >= 2:
                                if g == 2:
                                    dve.wait_ge(s["decay"], h + 1)
                                    dve.wait_ge(s["q"], G5 * h + (G5 + 2))
                                for t in range(*((0, 4), (4, 7), (7, 10))[g - 2]):
                                    ins = dve.tensor_scalar(KP[:, t, :], QE[:, j % 2, t, :], SK[:, t:t + 1], EPS0,
                                                            ALU.mult, ALU.add)
                                ins.then_inc(s["kp"], 3 if g == 2 else 1)

                for g in range(G5):
                    biases(0, 0, g)
                quad(0, True, False)
                with dve.Fori(1, QUADS - 1) as q:
                    quad(4 * q, False, False)
                quad(4 * (QUADS - 1), False, True)
                finish(HEADS0 - 1)


def cols_product(pe, k, w, src, chunks, outs, ready, freed, base=0):
    i = 0
    for f in range(outs):
        for lo, n in CHUNKS:
            if isinstance(base, int) and base == 0 and i < 2:
                pass
            else:
                pe.wait_ge(freed, base + i - 1)
            for c in range(chunks):
                mm = pe.matmul(k.PS[:, 4 + i % 2, 0:n], w[:, c, f * 128:(f + 1) * 128], src[:, c, lo:lo + n],
                               start=(c == 0), stop=(c == chunks - 1))
            mm.then_inc(ready, 1)
            i += 1


def mlp(nc, k, name, w1, b1, func, w2, b2, src, chunks, hidden, extra=None):
    loaded, made, stored, out, added, steps = (
        k.sem(f"{name}_{s}") for s in ("loaded", "hidden", "stored", "out", "added", "steps"))
    outs = hidden // 128
    with ExitStack() as ctx:
        A = ctx.enter_context(nc.sbuf_tensor(f"{name}_w1", [128, chunks, hidden], F32))
        B = ctx.enter_context(nc.sbuf_tensor(f"{name}_w2", [128, outs, D], F32))
        ba = ctx.enter_context(nc.sbuf_tensor(f"{name}_b1", [128, outs], F32))
        bb = ctx.enter_context(nc.sbuf_tensor(f"{name}_b2", [PT, D], F32))
        G = ctx.enter_context(nc.sbuf_tensor(f"{name}_h", [128, outs, N], F32))
        with nc.Block() as block:
            @block.sync
            def _(sp):
                sp.dma_start(A[:], chunks_of(w1)).then_inc(loaded, 16)
                sp.dma_start(B[:], chunks_of(w2)).then_inc(loaded, 16)
                with nc.allow_non_contiguous_dma(reason="one bias value per partition"):
                    sp.dma_start(ba[:], b1.rearrange("(k p) -> p k", p=128)).then_inc(loaded, 16)
                sp.dma_start(bb[:], spread(b2, D)).then_inc(loaded, 16)
                sp.wait_ge(loaded, 64)

            @block.tensor
            def _(pe):
                pe.wait_ge(loaded, 64)
                cols_product(pe, k, A, src, chunks, outs, made, stored)
                pe.wait_ge(stored, 3 * outs)
                rows_product(pe, k, G, B, outs, D, out, added)

            @block.scalar
            def _(act):
                act.wait_ge(loaded, 64)
                i = 0
                for f in range(outs):
                    for lo, n in CHUNKS:
                        act.wait_ge(made, i + 1)
                        act.activation(G[:, f, lo:lo + n], k.PS[:, 4 + i % 2, 0:n], func,
                                       bias=ba[:, f:f + 1]).then_inc(stored, 1)
                        i += 1

            @block.vector
            def _(dve):
                dve.wait_ge(loaded, 64)
                per = 2 + (extra is not None)
                link = Chain(dve, steps)
                for t in range(NT):
                    dve.wait_ge(out, t + 1)
                    ins = dve.tensor_tensor(halves(k.X[:, t, :]), pair_bank(k, t), halves(k.X[:, t, :]), ALU.add)
                    ins.then_inc(added, 1)
                    dve.wait_ge(added, t + 1)
                    link(dve.tensor_tensor(k.X[:, t, :], k.X[:, t, :], bb[:], ALU.add))
                    if extra is not None:
                        link(dve.tensor_tensor(k.X[:, t, :], k.X[:, t, :], extra[:, t, :], ALU.add))


def router(nc, k, name, gate, gate_bias, experts, top, b_proj, transposed):
    loaded, turned, gateT, scored, logits, steps, combT, comb_out, biased, expd, ct = (
        k.sem(f"{name}_{s}") for s in ("loaded", "turned", "gateT", "scored", "logits", "steps", "combT", "out",
                                        "biased", "exp", "ct"))
    with ExitStack() as ctx:
        sb = lambda n, sh, d=F32: ctx.enter_context(nc.sbuf_tensor(f"{name}_{n}", sh, d))
        gr, G = sb("gr", [experts, D]), sb("G", [128, KD, experts])
        LG, M8, I8, IF = sb("LG", [PT, NT, 8]), sb("M8", [PT, NT, 8]), sb("I8", [PT, NT, 8], U32), k.choice
        bg, bp = sb("bg", [PT, experts]), sb("bp", [experts, D])
        dl, w0, w1 = sb("dl", [PT, NT]), k.weight[:, 0, :], k.weight[:, 1, :]
        c1, CB = sb("c1", [PT, NT, 8]), sb("CB", [8, N])
        with nc.Block() as block:
            @block.sync
            def _(sp):
                if transposed:
                    sp.dma_start(gr[:], gate).then_inc(loaded, 16)
                else:
                    sp.dma_start(G[:], chunks_of(gate)).then_inc(loaded, 16)
                sp.dma_start(rows_of(k.rows_dram), k.XN[:]).then_inc(loaded, 16)
                if gate_bias is not None:
                    sp.dma_start(bg[:], spread(gate_bias, experts)).then_inc(loaded, 16)
                else:
                    sp.dma_start(bg[:, 0:1], spread(b_proj[0, 0:1], 1)).then_inc(loaded, 16)
                sp.dma_start(bp[:], b_proj).then_inc(loaded, 16)
                sp.wait_ge(loaded, 64)

            @block.tensor
            def _(pe):
                pe.wait_ge(loaded, 64)
                if transposed:
                    for c in range(KD):
                        mm = pe.transpose(k.PS[:, 7, c * experts:(c + 1) * experts], gr[:, c * 128:(c + 1) * 128],
                                          k.ident[0:experts, 0:experts])
                    mm.then_inc(turned, 1)
                    pe.wait_ge(gateT, 1)
                for t in range(NT):
                    for c in range(KD):
                        mm = pe.matmul(k.PS[0:PT, 6, t * 8:t * 8 + experts], k.FT[:, c, t * PT:(t + 1) * PT],
                                       G[:, c, :], start=(c == 0), stop=(c == KD - 1))
                mm.then_inc(scored, 1)
                pe.wait_ge(steps, 100)
                for t in range(NT):
                    mm = pe.transpose(k.PS[0:8, t // 4, (t % 4) * PT:(t % 4 + 1) * PT], k.comb[:, t, :],
                                      k.ident[0:PT, 0:PT])
                mm.then_inc(combT, 1)
                pe.wait_ge(ct, 1)
                for t in range(NT):
                    if t >= 2:
                        pe.wait_ge(biased, t - 1)
                    for h in range(2):
                        mm = pe.matmul(k.PS[0:PT, 2 * (t % 2) + h, 0:HALF], CB[0:experts, t * PT:(t + 1) * PT],
                                       bp[:, h * HALF:(h + 1) * HALF], start=True, stop=True)
                    mm.then_inc(comb_out, 1)

            @block.scalar
            def _(act):
                if top == 2:
                    act.wait_ge(logits, 2)
                    act.activation(w1, dl[:], ACT.Exp).then_inc(expd, 1)

            @block.vector
            def _(dve):
                dve.wait_ge(loaded, 64)
                link = Chain(dve, steps)
                if transposed:
                    dve.wait_ge(turned, 1)
                    dve.tensor_copy(G[:], k.PS[:, 7, 0:KD * experts].rearrange("p (c e) -> p c e", c=KD))\
                        .then_inc(gateT, 1)
                link(dve.memset(LG[:], -3.0e38))
                dve.wait_ge(scored, 1)
                ps = k.PS[0:PT, 6, 0:8 * NT].rearrange("p (t e) -> p t e", e=8)[:, :, 0:experts]
                if gate_bias is not None:
                    link(dve.tensor_tensor(LG[:, :, 0:experts], ps,
                                           bg[:].rearrange("p (o e) -> p o e", o=1).to_broadcast([PT, NT, experts]), ALU.add))
                else:
                    link(dve.tensor_copy(LG[:, :, 0:experts], ps))
                for t in range(NT):
                    link(dve.max(M8[:, t, :], LG[:, t, :]))
                    link(dve.max_index(I8[:, t, :], M8[:, t, :], LG[:, t, :]))
                link(dve.tensor_copy(IF[:], I8[:]))
                iota = k.iota8.rearrange("p (o e) -> p o e", o=1).to_broadcast([PT, NT, 8])
                col = lambda ap: ap.rearrange("p (t o) -> p t o", o=1)
                wide = lambda ap: col(ap).to_broadcast([PT, NT, 8])
                link(dve.tensor_tensor(k.comb[:], iota, IF[:, :, 0:1].to_broadcast([PT, NT, 8]), ALU.is_equal))
                if top == 2:
                    dve.tensor_tensor(col(dl[:]), M8[:, :, 1:2], M8[:, :, 0:1], ALU.subtract).then_inc(logits, 2)
                    dve.wait_ge(expd, 1)
                    link(dve.tensor_scalar(w0, w1, 1.0, None, ALU.add))
                    link(dve.reciprocal(w0, w0))
                    link(dve.tensor_tensor(w1, w1, w0, ALU.mult))
                    link(dve.tensor_tensor(c1[:], iota, IF[:, :, 1:2].to_broadcast([PT, NT, 8]), ALU.is_equal))
                    link(dve.tensor_tensor(c1[:], c1[:], wide(w1), ALU.mult))
                    link(dve.tensor_tensor(k.comb[:], k.comb[:], wide(w0), ALU.mult))
                    link(dve.tensor_tensor(k.comb[:], k.comb[:], c1[:], ALU.add))
                dve.nop().then_inc(steps, 100 - link.n)
                dve.wait_ge(combT, 1)
                for b, (lo, n) in enumerate(CHUNKS):
                    ins = dve.tensor_copy(CB[:, lo:lo + n], k.PS[0:8, b, 0:n])
                ins.then_inc(ct, 1)
                for t in range(NT):
                    dve.wait_ge(comb_out, t + 1)
                    dve.tensor_tensor(halves(k.X[:, t, :]), pair_bank(k, t), halves(k.X[:, t, :]), ALU.add)\
                        .then_inc(biased, 1)


def bin_items(nc, k, name, ids, columns, bins, group, groups, POS, BG):
    steps, counted, summed = (k.sem(f"{name}_{s}") for s in ("steps", "counted", "summed"))
    most = -(-columns * PT // group)
    with ExitStack() as ctx:
        sb = lambda n, sh, d=F32: ctx.enter_context(nc.sbuf_tensor(f"{name}_{n}", sh, d))
        hot, scan, zero = sb("hot", [PT, bins, columns]), sb("scan", [PT, bins, columns]), sb("zero", [PT, bins, columns])
        base, own, tot, ng, cum, off = (sb(n, [PT, bins]) for n in ("base", "own", "tot", "ng", "cum", "off"))
        more, late, place, bg = (sb("more", [PT, bins, most]), sb("late", [PT, groups, bins]),
                                 sb("place", [PT, columns]), sb("bg", [PT, groups]))
        with nc.Block() as block:
            @block.vector
            def _(dve):
                link = Chain(dve, steps)
                flat = lambda ap: ap.rearrange("p b c -> p (b c)")
                over_cols = lambda ap: ap.rearrange("p (b o) -> p b o", o=1).to_broadcast([PT, bins, columns])
                link(dve.memset(zero[:], 0.0))
                link(dve.tensor_tensor(hot[:], ids.rearrange("p (o c) -> p o c", o=1).to_broadcast([PT, bins, columns]),
                                       over_cols(k.iota[:, 0:bins]), ALU.is_equal))
                link(dve.tensor_tensor_scan(flat(scan[:]), flat(hot[:]), flat(zero[:]), 0.0, ALU.add, ALU.add))
                link(dve.memset(base[:], 0.0))
                link(dve.tensor_copy(base[:, 1:bins].rearrange("p (b o) -> p b o", o=1),
                                     scan[:, 0:bins - 1, columns - 1:columns]))
                link(dve.tensor_tensor(own[:].rearrange("p (b o) -> p b o", o=1), scan[:, :, columns - 1:columns],
                                       base[:].rearrange("p (b o) -> p b o", o=1), ALU.subtract))
                dve.nop().then_inc(counted, 1)
                dve.wait_ge(summed, 1)
                link(dve.tensor_copy(tot[:], k.PS[0:PT, 7, 64:64 + bins]))
                link(dve.tensor_scalar(more[:], k.iota[:, 0:most].rearrange("p (o j) -> p o j", o=1)
                                       .to_broadcast([PT, bins, most]), float(group), None, ALU.mult))
                link(dve.tensor_tensor(more[:], tot[:].rearrange("p (b o) -> p b o", o=1)
                                       .to_broadcast([PT, bins, most]), more[:], ALU.is_gt))
                link(dve.tensor_reduce(ng[:], more[:], AX.X, ALU.add))
                link(dve.tensor_tensor_scan(cum[:], ng[:], zero[:, 0, 0:bins], 0.0, ALU.add, ALU.add))
                link(dve.tensor_tensor(off[:], cum[:], ng[:], ALU.subtract))
                link(dve.tensor_scalar(off[:], off[:], float(group), -1.0, ALU.mult, ALU.add))
                link(dve.tensor_tensor(off[:], off[:], base[:], ALU.subtract))
                link(dve.tensor_tensor(off[:], off[:], k.PS[0:PT, 7, 0:bins], ALU.add))
                link(dve.tensor_tensor(scan[:], scan[:], over_cols(off[:]), ALU.add))
                link(dve.tensor_tensor(scan[:], scan[:], hot[:], ALU.mult))
                link(dve.tensor_reduce(place[:], scan[:].rearrange("p b c -> p c b"), AX.X, ALU.add))
                link(dve.tensor_copy(POS, place[:]))
                link(dve.tensor_tensor(late[:], k.iota[:, 0:groups].rearrange("p (g o) -> p g o", o=1)
                                       .to_broadcast([PT, groups, bins]),
                                       cum[:].rearrange("p (o b) -> p o b", o=1).to_broadcast([PT, groups, bins]),
                                       ALU.is_ge))
                link(dve.tensor_reduce(bg[:], late[:], AX.X, ALU.add))
                link(dve.tensor_scalar(BG, bg[:], float(bins - 1), None, ALU.min))

            @block.tensor
            def _(pe):
                pe.wait_ge(counted, 1)
                pe.matmul(k.PS[0:PT, 7, 0:bins], k.before[:], own[:], start=True, stop=True)
                pe.matmul(k.PS[0:PT, 7, 64:64 + bins], k.ones[0:PT, 0:PT], own[:], start=True, stop=True)\
                    .then_inc(summed, 1)


def list_items(nc, k, name, POS, columns, items, listed, groups, group_rows, LT):
    zeroed, cleared, back = (k.sem(f"{name}_{s}") for s in ("zeroed", "cleared", "back"))
    placed = k.gpsimd_dma_sem(f"{name}_placed")
    with ExitStack() as ctx:
        zero = ctx.enter_context(nc.sbuf_tensor(f"{name}_zero", [PT, groups], U32))
        with nc.Block() as block:
            @block.vector
            def _(dve):
                dve.memset(zero[:], 0).then_inc(zeroed, 1)

            @block.gpsimd
            def _(pool):
                pool.wait_ge(cleared, 16)
                for c in range(columns):
                    pool.indirect_dma_start(out=listed, out_offset=bass.IndirectOffsetOnAxis(ap=POS[:, c:c + 1], axis=0),
                                            in_=items(c), in_offset=None).then_inc(placed, 16)

            @block.sync
            def _(sp):
                sp.wait_ge(zeroed, 1)
                sp.dma_start(listed.rearrange("(p g) o -> p (g o)", p=PT), zero[:]).then_inc(cleared, 16)
                sp.wait_ge(placed, 16 * columns)
                with nc.allow_non_contiguous_dma(reason="a short list, one place per partition"):
                    sp.dma_start(LT, listed.rearrange("(g p) o -> p (g o)", p=group_rows)).then_inc(back, 16)
                sp.wait_ge(back, 16)


def load_experts(sp, w, W, loaded, experts):
    for e in range(experts):
        sp.dma_start(W[:, e, :, :], chunks_of(w[e, :, :])).then_inc(loaded, 16)


def experts_mlp(nc, k, name, b1, w2, experts, top, W1, w1_loaded, W2, w2_loaded):
    columns = top * NT
    groups = top * NT + experts - 1
    POS = k.POS[:, 0:columns]
    LT, BG = k.LT[:, 0:groups], k.BG[:, 0:groups]
    y_dram = k.expert_rows[0:groups * PT, :]
    listed = k.list_dram[0:groups * PT, :]
    k.ids_sem = k.sem(f"{name}_ids")
    with ExitStack() as ctx:
        ids = ctx.enter_context(nc.sbuf_tensor(f"{name}_ids", [PT, top, NT], F32))
        with nc.Block() as block:
            @block.sync
            def _(sp):
                load_experts(sp, w2, W2, w2_loaded, experts)

            @block.vector
            def _(dve):
                for j in range(top):
                    dve.tensor_copy(ids[:, j, :].rearrange("p (t o) -> p t o", o=1), k.choice[:, :, j:j + 1])\
                        .then_inc(k.ids_sem, 1)
        bin_items(nc, k, f"{name}_bin", ids[:].rearrange("p j t -> p (j t)"), columns, experts, PT, groups, POS, BG)
    list_items(nc, k, f"{name}_list", POS, columns, lambda c: k.node[:, c % NT:c % NT + 1], listed, groups, PT, LT)

    names = ("w2", "b", "gather", "xt", "xs", "h", "hb", "gt", "gs", "y", "ys", "out", "bc")
    s = {n: k.sem(f"{name}_{n}") for n in names}
    slot = {"gathered": [k.gpsimd_dma_sem(f"{name}_gathered{i}") for i in range(2)],
            "kept": [k.sem(f"{name}_kept{i}") for i in range(2)]}
    with ExitStack() as ctx:
        sb = lambda n, sh: ctx.enter_context(nc.sbuf_tensor(f"{name}_{n}", sh, F32))
        ba, bs = sb("b1", [128, experts, KF]), sb("bs", [128, 2, KF])
        XG, XT, HB, GT, Y = (sb("XG", [PT, 2, D]), sb("XT", [128, 2, KD, PT]), sb("HB", [PT, 2, F0]),
                             sb("GT", [128, 2, KF, PT]), sb("Y", [PT, 2, D]))
        with nc.Block() as block:
            @block.sync
            def _(sp):
                with nc.allow_non_contiguous_dma(reason="one bias value per partition"):
                    for e in range(experts):
                        sp.dma_start(ba[:, e, :], b1[e, :].rearrange("(k p) -> p k", p=128)).then_inc(s["b"], 16)
                for g in range(groups):
                    sp.wait_ge(s["ys"], g + 1)
                    sp.dma_start(y_dram[g * PT:(g + 1) * PT, :], Y[:, g % 2, :]).then_inc(slot["kept"][g % 2], 16)
                for i in range(2):
                    sp.wait_ge(slot["kept"][i], 16 * ((groups + 1 - i) // 2))

            @block.gpsimd
            def _(pool):
                for g in range(groups):
                    if g >= 2:
                        pool.wait_ge(s["xt"], g - 1)
                    pool.indirect_dma_start(out=XG[:, g % 2, :], out_offset=None, in_=k.rows_dram,
                                            in_offset=bass.IndirectOffsetOnAxis(ap=LT[:, g:g + 1], axis=0))\
                        .then_inc(slot["gathered"][g % 2], 16)

            @block.tensor
            def _(pe):
                def turn_rows(g, j):
                    pe.wait_ge(slot["gathered"][j % 2], 16 * (g // 2) + 16 if isinstance(g, int) else 8 * (g - j % 2) + 16)
                    if not (isinstance(g, int) and g < 1):
                        pe.wait_ge(s["xs"], g)
                    for c in range(KD):
                        mm = pe.transpose(k.PS[:, c // 3, (c % 3) * PT:(c % 3 + 1) * PT],
                                          XG[:, j % 2, c * 128:(c + 1) * 128], k.ident[0:PT, 0:PT])
                    mm.then_inc(s["xt"], 1)

                def up(g, j, e):
                    if isinstance(g, int) and g == 0:
                        pe.wait_ge(w1_loaded, 16 * experts)
                    pe.wait_ge(s["xs"], g + 1)
                    if not (isinstance(g, int) and g < 2):
                        pe.wait_ge(s["hb"], g - 1)
                    for c in range(KD):
                        mm = pe.matmul(k.PS[0:PT, 2 + j % 2, 0:F0], XT[:, j % 2, c, :],
                                       W1[:, bass.ds(e, 1), c, :].rearrange("p o n -> p (o n)"),
                                       start=(c == 0), stop=(c == KD - 1))
                    mm.then_inc(s["h"], 1)

                def turn_hidden(g, j):
                    pe.wait_ge(s["hb"], g + 1)
                    if not (isinstance(g, int) and g < 1):
                        pe.wait_ge(s["gs"], g)
                    for c in range(KF):
                        mm = pe.transpose(k.PS[:, 4, c * PT:(c + 1) * PT], HB[:, j % 2, c * 128:(c + 1) * 128],
                                          k.ident[0:PT, 0:PT])
                    mm.then_inc(s["gt"], 1)

                def down(g, j, e):
                    pe.wait_ge(s["gs"], g + 1)
                    if not (isinstance(g, int) and g < 1):
                        pe.wait_ge(s["ys"], g)
                    if isinstance(g, int) and g == 0:
                        pe.wait_ge(w2_loaded, 16 * experts)
                    for h in range(2):
                        for c in range(KF):
                            mm = pe.matmul(k.PS[0:PT, 5 + h, 0:HALF], GT[:, j % 2, c, :],
                                           W2[:, bass.ds(e, 1), c, h * HALF:(h + 1) * HALF].rearrange("p o n -> p (o n)"),
                                           start=(c == 0), stop=(c == KF - 1))
                    mm.then_inc(s["y"], 1)

                def expert_of(g):
                    return pe.value_load(BG[0:1, bass.ds(g, 1)], min_val=0, max_val=experts - 1)

                def step(g, j):
                    turn_rows(g + 1, j + 1)
                    up(g + 1, j + 1, expert_of(g + 1))
                    turn_hidden(g, j)
                    down(g, j, expert_of(g))

                turn_rows(0, 0)
                up(0, 0, expert_of(0))
                step(0, 0)
                step(1, 1)
                with pe.Fori(1, groups // 2) as couple:
                    for j in range(2):
                        step(2 * couple + j, j)
                if groups % 2 == 0:
                    raise ValueError("the last step of an even number of groups")
                turn_hidden(groups - 1, 0)
                down(groups - 1, 0, expert_of(groups - 1))

            @block.scalar
            def _(act):
                act.preload_act_table(ACT.Gelu)

                def rows(g, j):
                    act.wait_ge(s["xt"], g + 1)
                    if not (isinstance(g, int) and g < 2):
                        act.wait_ge(s["h"], g - 1)
                    act.activation(XT[:, j % 2, :, :].rearrange("p (a b) n -> p a b n", a=2),
                                   k.PS[:, 0:2, 0:3 * PT].rearrange("p a (b n) -> p a b n", b=3),
                                   ACT.Copy).then_inc(s["xs"], 1)

                def hidden(g, j):
                    act.wait_ge(s["gt"], g + 1)
                    act.wait_ge(s["bc"], g + 1)
                    if not (isinstance(g, int) and g < 2):
                        act.wait_ge(s["y"], g - 1)
                    for c in range(KF):
                        ins = act.activation(GT[:, j % 2, c, :], k.PS[:, 4, c * PT:(c + 1) * PT], ACT.Gelu,
                                             bias=bs[:, j % 2, c:c + 1])
                    ins.then_inc(s["gs"], 1)

                rows(0, 0)
                for g in range(2):
                    rows(g + 1, g + 1)
                    hidden(g, g)
                with act.Fori(1, groups // 2) as couple:
                    for j in range(2):
                        rows(2 * couple + j + 1, j + 1)
                        hidden(2 * couple + j, j)
                hidden(groups - 1, 0)

            @block.vector
            def _(dve):
                dve.wait_ge(s["b"], 16 * experts)

                def hidden(g, j):
                    e = dve.value_load(BG[0:1, bass.ds(g, 1)], min_val=0, max_val=experts - 1)
                    if not (isinstance(g, int) and g < 2):
                        dve.wait_ge(s["gs"], g - 1)
                    dve.tensor_copy(bs[:, j % 2, :], ba[:, bass.ds(e, 1), :].rearrange("p o c -> p (o c)"))\
                        .then_inc(s["bc"], 1)
                    dve.wait_ge(s["h"], g + 1)
                    if not (isinstance(g, int) and g < 2):
                        dve.wait_ge(s["gt"], g - 1)
                    dve.tensor_copy(HB[:, j % 2, :], k.PS[0:PT, 2 + j % 2, 0:F0]).then_inc(s["hb"], 1)

                def rows(g, j):
                    dve.wait_ge(s["y"], g + 1)
                    if not (isinstance(g, int) and g < 2):
                        dve.wait_ge(slot["kept"][j % 2], 16 * (g // 2) if isinstance(g, int) else 8 * (g - j % 2))
                    dve.tensor_copy(halves(Y[:, j % 2, :]), k.PS[0:PT, 5:7, 0:HALF]).then_inc(s["ys"], 1)

                hidden(0, 0)
                for g in range(2):
                    hidden(g + 1, g + 1)
                    rows(g, g)
                with dve.Fori(1, groups // 2) as couple:
                    for j in range(2):
                        hidden(2 * couple + j + 1, j + 1)
                        rows(2 * couple + j, j)
                rows(groups - 1, 0)


def combine_experts(nc, k, name, top):
    columns = top * NT
    got = [k.gpsimd_dma_sem(f"{name}_got{t}") for t in range(NT)]
    added = k.sem(f"{name}_added")
    with ExitStack() as ctx:
        YG = ctx.enter_context(nc.sbuf_tensor(f"{name}_YG", [PT, columns, D], F32))
        with nc.Block() as block:
            @block.gpsimd
            def _(pool):
                for c in range(columns):
                    t, j = c // top, c % top
                    pool.indirect_dma_start(out=YG[:, c, :], out_offset=None, in_=k.expert_rows,
                                            in_offset=bass.IndirectOffsetOnAxis(ap=k.POS[:, j * NT + t:j * NT + t + 1],
                                                                                axis=0)).then_inc(got[t], 16)

            @block.vector
            def _(dve):
                for c in range(columns):
                    t, j = c // top, c % top
                    dve.wait_ge(got[t], 16 * top)
                    if c >= 1:
                        dve.wait_ge(added, c)
                    w = k.weight[:, j, t:t + 1] if top == 2 else k.ones[0:PT, 0:1]
                    dve.scalar_tensor_tensor(out=k.X[:, t, :], in0=YG[:, c, :], scalar=w, in1=k.X[:, t, :],
                                             op0=ALU.mult, op1=ALU.add).then_inc(added, 1)


def mask(nc, k):
    turned, stored = k.sem("mask_turned"), k.sem("mask_stored")
    with nc.Block() as block:
        @block.tensor
        def _(pe):
            i = 0
            for d in range(NT):
                for g in range(0, NT, 4):
                    if i >= 2:
                        pe.wait_ge(stored, i - 1)
                    for s in range(g, min(g + 4, NT)):
                        mm = pe.transpose(k.PS[0:PT, i % 2, (s - g) * PT:(s - g + 1) * PT],
                                          k.CT[:, s, d * PT:(d + 1) * PT], k.ident[0:PT, 0:PT])
                    mm.then_inc(turned, 1)
                    i += 1

        @block.vector
        def _(dve):
            i = 0
            for d in range(NT):
                for lo, n in CHUNKS:
                    dve.wait_ge(turned, i + 1)
                    dve.tensor_scalar(k.MK[:, d, lo:lo + n], k.PS[0:PT, i % 2, 0:n], 0.5, NEG, ALU.is_lt, ALU.mult)\
                        .then_inc(stored, 1)
                    i += 1


def features(nc, k, name, src, chunks, w, hx, heads, width):
    loaded, made, stored, one = (k.sem(f"{name}_{s}") for s in ("loaded", "made", "stored", "one"))
    with ExitStack() as ctx:
        W = ctx.enter_context(nc.sbuf_tensor(f"{name}_W", [128, chunks, HID], F32))
        with nc.Block() as block:
            @block.sync
            def _(sp):
                sp.dma_start(W[:], chunks_of(w)).then_inc(loaded, 16)
                sp.wait_ge(loaded, 16)

            @block.gpsimd
            def _(pool):
                pool.memset(hx[:, :, :, width:width + 1], 1.0).then_inc(one, 1)

            @block.tensor
            def _(pe):
                pe.wait_ge(loaded, 16)
                for t in range(NT):
                    if t >= 2:
                        pe.wait_ge(stored, t - 1)
                    for c in range(chunks):
                        mm = pe.matmul(k.PS[0:PT, t % 2, 0:HID], src[:, c, t * PT:(t + 1) * PT], W[:, c, :],
                                       start=(c == 0), stop=(c == chunks - 1))
                    mm.then_inc(made, 1)

            @block.scalar
            def _(act):
                for t in range(NT):
                    act.wait_ge(made, t + 1)
                    act.activation(hx[:, t, :, 0:width], k.PS[0:PT, t % 2, 0:HID].rearrange("p (h d) -> p h d", h=heads),
                                   ACT.Copy).then_inc(stored, 1)


def gat(nc, k, name, a_src, a_dst, bias, hx, heads, width, dst):
    names = ("loaded", "steps", "rows", "rowsT", "spread", "spreadB", "maxed", "z", "brow", "browT", "b", "bB",
             "low", "lin", "e", "p", "sum", "out", "dd", "den")
    s = {n: k.sem(f"{name}_{n}") for n in names}
    parts = 1 if width * heads == HID and heads > 1 else 2
    span = N // parts
    W1 = width + 1
    per_bank = 5 if heads > 1 else 1
    banks = (NT // parts) // per_bank
    units = [(h, q) for h in range(heads) for q in range(parts)]
    with ExitStack() as ctx:
        sb = lambda n, sh, d=F32: ctx.enter_context(nc.sbuf_tensor(f"{name}_{n}", sh, d))
        av, bb = sb("av", [PT, 2, HID]), sb("bias", [PT, HID])
        tmp = sb("tmp", [PT, HID])
        AS, AD, MX, Z, LK = (sb(n, [PT, NT, heads]) for n in ("AS", "AD", "MX", "Z", "LK"))
        BB, AS2 = sb("BB", [PT, 2, NT, heads]), sb("AS2", [PT, NT, heads])
        spent = k.XN[:].rearrange("p t d -> p (t d)")[:, NT * HID:]
        low = spent[:, 0:2 * span].rearrange("p (s n) -> p s n", s=2)
        scrap, R = spent[:, 2 * N:3 * N], spent[0:8, 3 * N:4 * N]
        P = k.FT[0:PT, 2:5, 0:span]
        SB = sb("SB", [PT, 2, N])
        RD = sb("RD", [PT, NT])
        acc = lambda d: k.PS[0:PT, (d % (NT // parts)) // per_bank,
                             (d % per_bank) * W1:(d % per_bank + 1) * W1] if per_bank > 1 else \
            k.PS[0:PT, d % (NT // parts), 0:W1]
        with nc.Block() as block:
            @block.sync
            def _(sp):
                sp.dma_start(av[:, 0, :], a_src.rearrange("h d -> (h d)").rearrange("(a n) -> a n", a=1).to_broadcast([PT, HID])).then_inc(s["loaded"], 16)
                sp.dma_start(av[:, 1, :], a_dst.rearrange("h d -> (h d)").rearrange("(a n) -> a n", a=1).to_broadcast([PT, HID])).then_inc(s["loaded"], 16)
                sp.dma_start(bb[:], spread(bias, HID)).then_inc(s["loaded"], 16)
                sp.wait_ge(s["loaded"], 48)

            @block.vector
            def _(dve):
                link = Chain(dve, s["steps"])
                dve.wait_ge(s["loaded"], 48)
                hd = lambda ap: ap.rearrange("p (h d) -> p h d", h=heads)
                for t in range(NT):
                    for i, dest in enumerate((AS, AD)):
                        link(dve.tensor_tensor(hd(tmp[:]), hx[:, t, :, 0:width], hd(av[:, i, :]), ALU.mult))
                        link(dve.tensor_reduce(dest[:, t, :], hd(tmp[:]), AX.X, ALU.add))
                link(dve.tensor_scalar(AS2[:], AS[:], 0.2, None, ALU.mult))
                dve.nop().then_inc(s["rows"], 1)
                for b, (lo, n) in enumerate(CHUNKS):
                    if b == 0:
                        dve.wait_ge(s["rowsT"], 1)
                    ins = dve.tensor_copy(R[0:heads, lo:lo + n], k.PS[0:heads, b, 0:n])
                ins.then_inc(s["spread"], 1)
                for h in range(heads):
                    dve.wait_ge(s["spreadB"], h + 1)
                    for b, (lo, n) in enumerate(CHUNKS):
                        link(dve.tensor_copy(SB[:, 0, lo:lo + n], k.PS[0:PT, 3 + b, 0:n]))
                    for d in range(NT):
                        link(dve.tensor_tensor_reduce(scrap[:], k.MK[:, d, :], SB[:, 0, :], 1.0, -3.0e38,
                                                      ALU.add, ALU.max, MX[:, d, h:h + 1]))
                    dve.nop().then_inc(s["maxed"], 1)
                link(dve.tensor_tensor(Z[:], AD[:], MX[:], ALU.add))
                link(dve.tensor_scalar(LK[:], Z[:], 0.2, None, ALU.mult))
                link(dve.tensor_tensor(Z[:], Z[:], LK[:], ALU.max))
                link(dve.tensor_tensor(BB[:, 0], AD[:], Z[:], ALU.subtract))
                link(dve.scalar_tensor_tensor(out=BB[:, 1], in0=AD[:], scalar=0.2, in1=Z[:], op0=ALU.mult,
                                              op1=ALU.subtract))
                dve.nop().then_inc(s["z"], 1)

            @block.tensor
            def _(pe):
                pe.wait_ge(s["rows"], 1)
                for t in range(NT):
                    mm = pe.transpose(k.PS[0:heads, t // 4, (t % 4) * PT:(t % 4 + 1) * PT], AS[:, t, :],
                                      k.ident[0:PT, 0:PT])
                mm.then_inc(s["rowsT"], 1)
                pe.wait_ge(s["spread"], 1)
                for h in range(heads):
                    if h:
                        pe.wait_ge(s["maxed"], h)
                    for b, (lo, n) in enumerate(CHUNKS):
                        mm = pe.matmul(k.PS[0:PT, 3 + b, 0:n], k.sel[0:heads, h, :], R[0:heads, lo:lo + n],
                                       start=True, stop=True)
                    mm.then_inc(s["spreadB"], 1)
        R2 = sb("R2", [8, N])
        with nc.Block() as block:
            @block.tensor
            def _(pe):
                for i in range(2):
                    for t in range(NT):
                        mm = pe.transpose(k.PS[0:heads, 3 * i + t // 4, (t % 4) * PT:(t % 4 + 1) * PT],
                                          BB[:, i, t, :], k.ident[0:PT, 0:PT])
                mm.then_inc(s["browT"], 1)

            @block.vector
            def _(dve):
                dve.wait_ge(s["browT"], 1)
                for i, dest in enumerate((R, R2)):
                    for b, (lo, n) in enumerate(CHUNKS):
                        dve.tensor_copy(dest[0:heads, lo:lo + n], k.PS[0:heads, 3 * i + b, 0:n]).then_inc(s["brow"], 1)
        for u, (h, q) in enumerate(units):
            if q == 0:
                with nc.Block() as block:
                    @block.tensor
                    def _(pe):
                        for i, row in enumerate((R, R2)):
                            for b, (lo, n) in enumerate(CHUNKS):
                                mm = pe.matmul(k.PS[0:PT, 3 * i + b, 0:n], k.sel[0:heads, h, :], row[0:heads, lo:lo + n],
                                               start=True, stop=True)
                        mm.then_inc(s["b"], 1)

                    @block.vector
                    def _(dve):
                        dve.wait_ge(s["b"], h + 1)
                        for i in range(2):
                            for b, (lo, n) in enumerate(CHUNKS):
                                dve.tensor_copy(SB[:, i, lo:lo + n], k.PS[0:PT, 3 * i + b, 0:n]).then_inc(s["bB"], 1)
            with nc.Block() as block:
                lo = q * span
                tiles = range(q * (NT // parts), (q + 1) * (NT // parts))
                g0 = u * NT

                @block.scalar
                def _(act):
                    def lower(t):
                        if g0 + t >= 2:
                            act.wait_ge(s["lin"], g0 + t - 1)
                        act.activation(low[:, (g0 + t) % 2, :], SB[:, 1, lo:lo + span], ACT.Identity,
                                       bias=AS2[:, t, h:h + 1]).then_inc(s["low"], 1)
                    lower(0)
                    for t in range(NT):
                        if t + 1 < NT:
                            lower(t + 1)
                        act.wait_ge(s["lin"], g0 + t + 1)
                        act.activation(P[:, (g0 + t) % 3, :], P[:, (g0 + t) % 3, :], ACT.Exp).then_inc(s["e"], 1)

                @block.vector
                def _(dve):
                    def linear(t):
                        dve.wait_ge(s["low"], g0 + t + 1)
                        if g0 + t >= 3:
                            dve.wait_ge(s["sum"], g0 + t - 2)
                        dve.scalar_tensor_tensor(out=P[:, (g0 + t) % 3, :], in0=SB[:, 0, lo:lo + span],
                                                 scalar=AS[:, t, h:h + 1], in1=low[:, (g0 + t) % 2, :],
                                                 op0=ALU.add, op1=ALU.max).then_inc(s["lin"], 1)
                    linear(0)
                    for t in range(NT):
                        if t + 1 < NT:
                            linear(t + 1)
                        dve.wait_ge(s["e"], g0 + t + 1)
                        pt = P[:, (g0 + t) % 3, :]
                        dve.tensor_tensor(pt, pt, k.CT[:, t, lo:lo + span], ALU.mult).then_inc(s["p"], 1)
                    dve.wait_ge(s["sum"], g0 + NT)
                    nt = NT // parts
                    if per_bank > 1:
                        A = k.PS[0:PT, 0:banks, 0:per_bank * W1].rearrange("p b (c d) -> p b c d", d=W1)
                    else:
                        A = k.PS[0:PT, 0:banks, 0:W1].rearrange("p b (c d) -> p b c d", c=1)
                    rd = RD[:, 0:nt].rearrange("p (b c o) -> p b c o", b=banks, o=1)
                    link = Chain(dve, s["den"], 4 * u)
                    link(dve.tensor_scalar(rd, A[:, :, :, width:W1], 1e-16, None, ALU.add))
                    link(dve.reciprocal(rd, rd))
                    ov = dst[:, tiles[0]:tiles[-1] + 1, h * width:(h + 1) * width].rearrange(
                        "p (b c) d -> p b c d", b=banks)
                    link(dve.tensor_tensor(ov, A[:, :, :, 0:width], rd.to_broadcast([PT, banks, per_bank, width]), ALU.mult))
                    ov3 = dst[:, tiles[0]:tiles[-1] + 1, h * width:(h + 1) * width]
                    link(dve.tensor_tensor(ov3, ov3, bb[:, h * width:(h + 1) * width].rearrange("p (o d) -> p o d", o=1)
                                           .to_broadcast([PT, nt, width]), ALU.add))
                    dve.tensor_scalar(ov3, ov3, 0.0, None, ALU.max).then_inc(s["out"], 1)

                @block.tensor
                def _(pe):
                    for t in range(NT):
                        pe.wait_ge(s["p"], g0 + t + 1)
                        for i, d in enumerate(tiles):
                            mm = pe.matmul(acc(d), P[:, (g0 + t) % 3, i * PT:(i + 1) * PT],
                                           hx[:, t, h, :], start=(t == 0 and i % per_bank == 0), stop=(t == NT - 1),
                                           skip_group_check=True)
                        mm.then_inc(s["sum"], 1)


def linear_mixer(nc, k, a):
    names = ("wk", "wv", "wq", "wp", "ga", "k", "kf", "ks", "kr", "kst", "v", "vf", "kv", "kvt", "kvB", "q", "qf", "steps", "qs",
             "qr", "std", "n", "turned", "stored", "y", "added", "kvs")
    s = {n: k.sem(f"lin_{n}") for n in names}
    third = lambda i: chunks_of(a["L1_mix_w_qkv"])[:, :, i * D:(i + 1) * D]
    with ExitStack() as ctx:
        sb = lambda n, sh: ctx.enter_context(nc.sbuf_tensor(f"lin_{n}", sh, F32))
        W = sb("W", [128, KD, D])
        gb = sb("gb", [PT, 2, D])
        kv, kvB, sqj = sb("kv", [PT, 2, D]), sb("kvB", [PT, D]), sb("sqj", [PT, 2, HALF])
        ss, rn = sb("ss", [PT, NT]), sb("rn", [PT, NT])
        st, mv, sd, rs = sb("st", [PT, NT, 2, 6]), sb("mv", [PT, NT, 2]), sb("sd", [PT, NT]), sb("rs", [PT, NT])

        def norms(name, dst, save):
            with nc.Block() as block:
                @block.sync
                def _(sp):
                    sp.dma_start(W[:], third({"k": 1, "q": 0}[name])).then_inc(s["w" + name], 16)
                    sp.wait_ge(s["w" + name], 16)
                    if name == "q":
                        sp.dma_start(gb[:, 0, :], spread(a["L1_mix_ln_out_g"], D)).then_inc(s["ga"], 16)
                        sp.dma_start(gb[:, 1, :], spread(a["L1_mix_ln_out_b"], D)).then_inc(s["ga"], 16)
                        sp.wait_ge(s["ga"], 32)

                @block.tensor
                def _(pe):
                    pe.wait_ge(s["w" + name], 16)
                    rows_product(pe, k, k.FT, W, KD, D, s[name], s[name + "f"])

                @block.scalar
                def _(act):
                    for t in range(NT):
                        act.wait_ge(s[name], t + 1)
                        if t:
                            act.wait_ge(s[name + "s"], t)
                        act.activation(sqj[:], pair_bank(k, t), ACT.Square, accum_out=ss[:, t:t + 1]).then_inc(s[name + "s"], 1)
                        act.activation(halves(dst[:, t, :]), pair_bank(k, t), ACT.Copy).then_inc(s[name + "f"], 1)
                    act.wait_ge(s[name + "s"], NT)
                    act.activation(rn[:], ss[:], ACT.Sqrt).then_inc(s[name + "r"], 1)

                @block.vector
                def _(dve):
                    dve.wait_ge(s[name + "r"], 1)
                    dve.tensor_scalar(rn[:], rn[:], 1e-12, None, ALU.max).then_inc(s[name + "r"], 1)
                    dve.wait_ge(s[name + "r"], 2)
                    dve.reciprocal(rn[:], rn[:]).then_inc(s[name + "r"], 1)

        norms("k", k.XN, True)
        with nc.Block() as block:
            @block.sync
            def _(sp):
                sp.dma_start(W[:], third(2)).then_inc(s["wv"], 16)
                sp.wait_ge(s["wv"], 16)

            @block.tensor
            def _(pe):
                pe.wait_ge(s["wv"], 16)
                for t in range(NT + 1):
                    if t < NT:
                        if t >= 2:
                            pe.wait_ge(s["vf"], t - 1)
                        for h in range(2):
                            for c in range(KD):
                                mm = pe.matmul(k.PS[0:PT, 2 * (t % 2) + h, 0:HALF], k.FT[:, c, t * PT:(t + 1) * PT],
                                               W[:, c, h * HALF:(h + 1) * HALF], start=(c == 0), stop=(c == KD - 1))
                        mm.then_inc(s["v"], 1)
                    if t >= 1:
                        pe.wait_ge(s["vf"], t)
                        for h in range(2):
                            mm = pe.matmul(k.PS[0:PT, 4 + h, 0:HALF], k.ones[0:PT, 0:PT],
                                           kv[:, (t - 1) % 2, h * HALF:(h + 1) * HALF], start=(t == 1), stop=(t == NT))
                        mm.then_inc(s["kvt"], 1)

            @block.vector
            def _(dve):
                for t in range(NT):
                    dve.wait_ge(s["v"], t + 1)
                    if t >= 2:
                        dve.wait_ge(s["kvt"], t - 1)
                    dve.scalar_tensor_tensor(out=halves(kv[:, t % 2, :]), in0=pair_bank(k, t), scalar=rn[:, t:t + 1],
                                             in1=halves(k.XN[:, t, :]), op0=ALU.mult, op1=ALU.mult).then_inc(s["vf"], 1)
                dve.wait_ge(s["kvt"], NT)
                dve.tensor_copy(halves(kvB[:]), k.PS[0:PT, 4:6, 0:HALF]).then_inc(s["kvB"], 1)
        norms("q", k.XN, True)
        with nc.Block() as block:
            @block.vector
            def _(dve):
                for t in range(NT):
                    dve.scalar_tensor_tensor(out=k.XN[:, t, :], in0=k.XN[:, t, :], scalar=rn[:, t:t + 1], in1=kvB[:],
                                             op0=ALU.mult, op1=ALU.mult).then_inc(s["n"], 1)
    layernorm(nc, k, "lno", k.XN, k.XN, a["L1_mix_ln_out_g"], a["L1_mix_ln_out_b"])
    with ExitStack() as ctx:
        W = ctx.enter_context(nc.sbuf_tensor("lin_Wp", [128, KD, D], F32))
        with nc.Block() as block:
            @block.sync
            def _(sp):
                sp.dma_start(W[:], chunks_of(a["L1_mix_w_proj"])).then_inc(s["wp"], 16)
                sp.wait_ge(s["wp"], 16)

            @block.tensor
            def _(pe):
                pe.wait_ge(s["wp"], 16)
                rows_product(pe, k, k.FT, W, KD, D, s["y"], s["added"])

            @block.vector
            def _(dve):
                for t in range(NT):
                    dve.wait_ge(s["y"], t + 1)
                    dve.tensor_tensor(halves(k.X[:, t, :]), pair_bank(k, t), halves(k.X[:, t, :]), ALU.add)\
                        .then_inc(s["added"], 1)


def store(nc, k, out):
    stored = k.sem("x_stored")
    with nc.Block() as block:
        @block.sync
        def _(sp):
            sp.dma_start(rows_of(out), k.X[:]).then_inc(stored, 16)
            sp.wait_ge(stored, 16)


def program(nc, a, out):
    with ExitStack() as ctx:
        sb = lambda n, s, d=F32: ctx.enter_context(nc.sbuf_tensor(n, s, d))
        k = Kit()
        k.nc, k.sems = nc, []
        k.PS = ctx.enter_context(nc.psum_tensor("PS", [128, 8, 512], F32))
        k.X = sb("X", [PT, NT, D])
        k.choice = sb("choice", [PT, NT, 8])
        k.weight = sb("weight", [PT, 2, NT])
        k.POS, k.LT, k.BG = sb("POS", [PT, 2 * NT], U32), sb("LT", [PT, MOST], U32), sb("BG", [PT, MOST], I32)

        def norm_room(c, part):
            k.XN = c.enter_context(nc.sbuf_tensor(f"XN_{part}", [PT, NT, D], F32))
            k.FT = c.enter_context(nc.sbuf_tensor(f"FT_{part}", [128, KD, N], F32))
        k.ident, k.ones = sb("ident", [128, 128]), sb("ones", [128, 128])
        k.sel, k.iota = sb("sel", [8, 8, PT]), sb("iota", [PT, 64])
        k.iota8, k.before, k.node = k.iota[:, 0:8], sb("before", [PT, PT]), sb("node", [PT, NT], U32)
        k.comb, k.scrap = sb("comb", [PT, NT, 8]), sb("scrap", [1, 8])
        k.ln_eps = sb("ln_eps", [128, 1])
        epsd = k.sem("eps_made")
        with nc.Block() as block:
            @block.vector
            def _(dve):
                dve.memset(k.ln_eps[:], LN_EPS).then_inc(epsd, 1)
        setup(nc, k, a)

        with ExitStack() as c0:
            k.KEY, k.EPOS = (c0.enter_context(nc.sbuf_tensor(n, [PT, EC], U32)) for n in ("KEY", "EPOS"))
            k.ETILE = c0.enter_context(nc.sbuf_tensor("ETILE", [PT, EGROUPS], I32))
            with ExitStack() as c1:
                norm_room(c1, "layer0")
                layernorm(nc, k, "ln0", k.X, k.XN)
                gcn_features(nc, k, a)
                place_edges(nc, k, a)
                clear_edge_list(nc, k)
                with ExitStack() as c2:
                    k.HV = c2.enter_context(nc.sbuf_tensor("HV", [PT, NT, HEADS0, DH0 + 1], F32))
                    with ExitStack() as c3:
                        H = c3.enter_context(nc.sbuf_tensor("H", [PT, NT, D], F32))
                        layernorm(nc, k, "ln1", k.XN, H, a["L0_mix_ln1_g"], a["L0_mix_ln1_b"], spare=k.HV)
                    k.recycle()
                    k.pdup = c2.enter_context(nc.sbuf_tensor("pdup", [128, 2, 2, DH0], F32))
                    favor(nc, k, a, background=scatter_edges(nc, k))
                with ExitStack() as c2:
                    H = c2.enter_context(nc.sbuf_tensor("H2", [PT, NT, D], F32))
                    layernorm(nc, k, "ln2", k.XN, H, a["L0_mix_ln2_g"], a["L0_mix_ln2_b"])
                    mlp(nc, k, "ffn0", a["L0_mix_W1"], a["L0_mix_b1"], ACT.Gelu, a["L0_mix_W2"], a["L0_mix_b2"],
                        k.FT, KD, F0, extra=k.XN)
            k.CT = c0.enter_context(nc.sbuf_tensor("CT", [PT, NT, N], F32))
            k.recycle()
            HS = c0.enter_context(nc.sbuf_tensor("HS", [PT, NT, D], F32))
            count_edges(nc, k, HS)
            gcn(nc, k, a, HS)
            saved = k.sem("counts_saved")
            with nc.Block() as block:
                @block.sync
                def _(sp):
                    sp.dma_start(k.counts, k.CT[:]).then_inc(saved, 16)
                    sp.wait_ge(saved, 16)
        k.recycle()

        def mixture(name, ln, gate, gate_bias, experts, top, w1, b1, w2, b2, transposed):
            with ExitStack() as c1:
                W1 = c1.enter_context(nc.sbuf_tensor(f"{name}_W1", [128, experts, KD, F0], F32))
                w1_loaded = k.sem(f"{name}_w1_loaded")
                with nc.Block() as block:
                    @block.sync
                    def _(sp):
                        load_experts(sp, w1, W1, w1_loaded, experts)
                with ExitStack() as c2:
                    norm_room(c2, name)
                    layernorm(nc, k, ln, k.X, k.XN)
                    router(nc, k, f"{name}_rt", gate, gate_bias, experts, top, b2, transposed)
                W2 = c1.enter_context(nc.sbuf_tensor(f"{name}_W2", [128, experts, KF, D], F32))
                experts_mlp(nc, k, name, b1, w2, experts, top, W1, w1_loaded, W2, k.sem(f"{name}_w2_loaded"))
            k.recycle()
            combine_experts(nc, k, f"{name}_sum", top)

        mixture("moe0", "ln3", a["L0_ffn_router_w"], None, EXP0, 2, a["L0_ffn_w_fc"], a["L0_ffn_b_fc"],
                a["L0_ffn_w_proj"], a["L0_ffn_b_proj"], True)

        k.recycle()
        with ExitStack() as c1:
            norm_room(c1, "layer1")
            layernorm(nc, k, "ln4", k.X, k.XN)
            with ExitStack() as c2:
                hx = c2.enter_context(nc.sbuf_tensor("hx1", [PT, NT, HEADS1, HID // HEADS1 + 1], F32))
                features(nc, k, "ft1", k.FT, KD, a["L1_gnn_W1"], hx, HEADS1, HID // HEADS1)
                with ExitStack() as c3:
                    layernorm(nc, k, "ln5", k.XN, k.XN, a["L1_mix_ln_in_g"], a["L1_mix_ln_in_b"])
                    linear_mixer(nc, k, a)
                k.recycle()
                G1 = k.XN[:].rearrange("p t d -> p (t d)")[:, 0:NT * HID].rearrange("p (t d) -> p t d", t=NT)
                GT = k.FT[:, 0:2, :]
                k.CT = c2.enter_context(nc.sbuf_tensor("CTb", [PT, NT, N], F32))
                back = k.sem("counts_back")
                with nc.Block() as block:
                    @block.sync
                    def _(sp):
                        sp.dma_start(k.CT[:], k.counts).then_inc(back, 16)
                        sp.wait_ge(back, 16)
                k.MK = c2.enter_context(nc.sbuf_tensor("MK", [PT, NT, N], BF16))
                mask(nc, k)
                with ExitStack() as c3:
                    gat(nc, k, "gat1", a["L1_gnn_a_src1"], a["L1_gnn_a_dst1"], a["L1_gnn_b1"], hx, HEADS1,
                        HID // HEADS1, G1)
                turn(nc, k, "tn1", G1, GT, 2)
                hx2 = hx[:].rearrange("p t h d -> p t (h d)")[:, :, 0:HID + 1].rearrange("p t (o d) -> p t o d", o=1)
                features(nc, k, "ft2", GT, 2, a["L1_gnn_W2"], hx2, 1, HID)
                gat(nc, k, "gat2", a["L1_gnn_a_src2"], a["L1_gnn_a_dst2"], a["L1_gnn_b2"], hx2, 1, HID, G1)
                turn(nc, k, "tn2", G1, GT, 2)
                mlp(nc, k, "gmlp", a["L1_gnn_Wm1"], a["L1_gnn_bm1"], ACT.Relu, a["L1_gnn_Wm2"], a["L1_gnn_bm2"],
                    GT, 2, HID)
        k.recycle()
        mixture("moe1", "ln6", a["L1_ffn_Wg"], a["L1_ffn_bg"], EXP1, 1, a["L1_ffn_W1"], a["L1_ffn_b1"],
                a["L1_ffn_W2"], a["L1_ffn_b2"], False)
        store(nc, k, out)


def kernel(**inputs):
    import numpy as np
    import concourse.bacc as bacc
    from concourse.bass_utils import run_bass_kernel_spmd as run

    nc = bacc.Bacc("TRN2", target_bir_lowering=False, num_devices=1)
    arrays, a = {}, {}
    for name, value in inputs.items():
        v = np.ascontiguousarray(value)
        arrays["in_" + name] = v
        a[name] = nc.dram_tensor("in_" + name, v.shape, mybir.dt.from_np(v.dtype), kind="ExternalInput").ap()
    out = nc.dram_tensor("out", (N, D), F32, kind="ExternalOutput").ap()
    Kit.rows_dram = nc.dram_tensor("normal_rows", (N, D), F32, kind="Internal").ap()
    Kit.expert_rows = nc.dram_tensor("expert_rows", (MOST * PT, D), F32, kind="Internal").ap()
    Kit.list_dram = nc.dram_tensor("node_list", (MOST * PT, 1), U32, kind="Internal").ap()
    Kit.edge_list = nc.dram_tensor("edge_list", (EGROUPS * EGROUP, 1), U32, kind="Internal").ap()
    Kit.features = nc.dram_tensor("gcn_features", (N, D), F32, kind="Internal").ap()
    Kit.counts = nc.dram_tensor("counts", (PT, NT, N), F32, kind="Internal").ap()
    program(nc, a, out)
    r = run(nc, [arrays], core_ids=[0])
    return r.results[0]["out"]
```
